# Optimizing a Trainium2 kernel written in Bass

```python
import numpy as np
import jax
import jax.numpy as jnp

def _softmax(x, axis=-1):
    return jax.nn.softmax(x, axis=axis)

def _gelu(x):
    return jax.nn.gelu(x, approximate=True)

def _silu(x):
    return jax.nn.silu(x)

def _sigmoid(x):
    return jax.nn.sigmoid(x)

def _layernorm(x, axis=-1, eps=1e-05):
    m = jnp.mean(x, axis=axis, keepdims=True)
    v = jnp.var(x, axis=axis, keepdims=True)
    return (x - m) / jnp.sqrt(v + eps)

def _scatter_add(tgt, idx, src, axis=0):
    return tgt.at[idx].add(src)

def _segment_sum(src, seg, n):
    return jax.ops.segment_sum(src, seg, n)
kernel_name = 'mk_adaln_ffn_d2_seqx_r8_b5ac9a'

def setup_inputs(seed: int=0):
    np.random.seed(seed)
    _w = jnp.asarray

    def _rec_inputs():
        import jax
        import jax.numpy as jnp
        _rk = jax.random.key(seed)
        x = -0.000125 + 0.9999 * jax.random.normal(jax.random.fold_in(_rk, 1), (32, 32, 256), jnp.float32)
        _lenS = 32 - jax.random.randint(jax.random.fold_in(_rk, 7), (32,), 0, max(1, 32 // 4) + 1, jnp.int32)
        _lenS2 = 32 - jax.random.randint(jax.random.fold_in(_rk, 8), (32,), 0, max(1, 32 // 4) + 1, jnp.int32)
        itok_B_0_7 = jax.random.randint(jax.random.fold_in(_rk, 11), (32,), 0, 8, jnp.int32)
        fside_8xS_0 = -0.00162727 + 0.0609077 * jax.random.normal(jax.random.fold_in(_rk, 12), (8, 32), jnp.float32)
        itok_B_1_198 = jax.random.randint(jax.random.fold_in(_rk, 13), (32,), 1, 199, jnp.int32)
        return (x, itok_B_0_7, fside_8xS_0, itok_B_1_198)
    x, itok_B_0_7, fside_8xS_0, itok_B_1_198 = _rec_inputs()

    def _L0_cond_setup():
        import jax, jax.numpy as jnp
        import numpy as np
        B, C, T = (64, 32, 256)
        D, N = (32, 8)
        key = jax.random.key(seed)
        k_x, k_s, k_w, k_b = jax.random.split(key, 4)
        scale = 1.0 / np.sqrt(C)
        x = jax.random.normal(k_x, (B, C, T), dtype=jnp.float32)
        subjects = jax.random.randint(k_s, (B,), 0, N, dtype=jnp.int64)
        weights = jax.random.normal(k_w, (N, C, D), dtype=jnp.float32) * scale
        bias = jax.random.normal(k_b, (N, D), dtype=jnp.float32) * scale
        return {'x': x, 'subjects': subjects, 'weights': weights, 'bias': bias}
    _L0_cond_all = _L0_cond_setup()
    _L0_cond_in = {k: v for k, v in _L0_cond_all.items() if k in ('weights',)}
    del _L0_cond_all

    def _L0_ffn_setup():
        import jax, jax.numpy as jnp
        import numpy as np
        DIM = 256
        INNER = 1024
        EPS_RMS = 1e-06
        EPS_Q = 1e-05

        def simple_rms_norm(x, dim):
            rms = jnp.sqrt(jnp.mean(x * x, axis=-1, keepdims=True) + EPS_RMS)
            return x / rms * dim ** (-0.5)

        def activation_quant(x):
            scale = 127.0 / jnp.clip(jnp.max(jnp.abs(x), axis=-1, keepdims=True), EPS_Q)
            return jnp.clip(jnp.round(x * scale), -128, 127) / scale

        def weight_quant(w):
            return jnp.sign(w) * jnp.mean(jnp.abs(w))

        def bit_linear(x, w, b, dim_in):
            x_norm = simple_rms_norm(x, dim_in)
            x_q = activation_quant(x_norm)
            w_q = weight_quant(w)
            return jnp.einsum('bsd,od->bso', x_q, w_q) + b
        key = jax.random.key(seed)
        k1, k2, k3, k4, k5 = jax.random.split(key, 5)
        bound1 = 1.0 / np.sqrt(DIM)
        bound2 = 1.0 / np.sqrt(INNER)
        return {'x': jax.random.normal(k1, (4, 256, DIM), dtype=jnp.float32), 'w1': jax.random.uniform(k2, (INNER, DIM), jnp.float32, -bound1, bound1), 'b1': jax.random.uniform(k3, (INNER,), jnp.float32, -bound1, bound1), 'w2': jax.random.uniform(k4, (DIM, INNER), jnp.float32, -bound2, bound2), 'b2': jax.random.uniform(k5, (DIM,), jnp.float32, -bound2, bound2)}
    _L0_ffn_all = _L0_ffn_setup()
    _L0_ffn_in = {k: v for k, v in _L0_ffn_all.items() if k in ('w1', 'b1', 'w2', 'b2')}
    del _L0_ffn_all

    def _L1_cond_setup():
        import jax, jax.numpy as jnp
        import numpy as np
        B, C, T = (128, 32, 256)
        S, D = (200, 32)
        key = jax.random.key(seed)
        k1, k2, k3 = jax.random.split(key, 3)
        x = jax.random.normal(k1, (B, C, T), dtype=jnp.float32)
        conditions = jax.random.randint(k2, (B,), 0, S, dtype=jnp.int64)
        weights = jax.random.normal(k3, (S, C, D), dtype=jnp.float32) / jnp.sqrt(jnp.float32(C))
        return {'x': x, 'conditions': conditions, 'weights': weights}
    _L1_cond_all = _L1_cond_setup()
    _L1_cond_in = {k: v for k, v in _L1_cond_all.items() if k in ('weights',)}
    del _L1_cond_all

    def _L1_ffn_setup():
        import jax, jax.numpy as jnp
        import numpy as np
        B, S, D, F, E, SH, K = (2, 256, 256, 128, 16, 2, 2)

        def _experts_all(x, g, gb, w1, b1, w2, b2):
            y = jax.nn.gelu(jnp.einsum('bsd,edf->bsef', x, g) + gb, approximate=False)
            y = y * (jnp.einsum('bsd,edf->bsef', x, w1) + b1)
            return jnp.einsum('bsef,efd->bsed', y, w2) + b2
        key = jax.random.key(seed)
        ks = jax.random.split(key, 8)
        std = 0.02
        mk = lambda k, sh: jax.random.normal(k, sh, jnp.float32) * std
        return {'x': jax.random.normal(ks[0], (B, S, D), jnp.float32), 'wa': mk(ks[1], (D, E)), 'rg': mk(ks[2], (E, D, F)), 'rgb': jnp.zeros((E, F), jnp.float32), 'rw1': mk(ks[3], (E, D, F)), 'rb1': jnp.zeros((E, F), jnp.float32), 'rw2': mk(ks[4], (E, F, D)), 'rb2': jnp.zeros((E, D), jnp.float32), 'sg': mk(ks[5], (SH, D, F)), 'sgb': jnp.zeros((SH, F), jnp.float32), 'sw1': mk(ks[6], (SH, D, F)), 'sb1': jnp.zeros((SH, F), jnp.float32), 'sw2': mk(ks[7], (SH, F, D)), 'sb2': jnp.zeros((SH, D), jnp.float32)}
    _L1_ffn_all = _L1_ffn_setup()
    _L1_ffn_in = {k: v for k, v in _L1_ffn_all.items() if k in ('wa', 'rg', 'rgb', 'rw1', 'rb1', 'rw2', 'rb2', 'sg', 'sgb', 'sw1', 'sb1', 'sw2', 'sb2')}
    del _L1_ffn_all
    return {'x': x, 'itok_B_0_7': itok_B_0_7, 'fside_8xS_0': fside_8xS_0, 'itok_B_1_198': itok_B_1_198, 'L0_cond_weights': _L0_cond_in['weights'], 'L0_ffn_w1': _L0_ffn_in['w1'], 'L0_ffn_b1': _L0_ffn_in['b1'], 'L0_ffn_w2': _L0_ffn_in['w2'], 'L0_ffn_b2': _L0_ffn_in['b2'], 'L1_cond_weights': _L1_cond_in['weights'], 'L1_ffn_wa': _L1_ffn_in['wa'], 'L1_ffn_rg': _L1_ffn_in['rg'], 'L1_ffn_rgb': _L1_ffn_in['rgb'], 'L1_ffn_rw1': _L1_ffn_in['rw1'], 'L1_ffn_rb1': _L1_ffn_in['rb1'], 'L1_ffn_rw2': _L1_ffn_in['rw2'], 'L1_ffn_rb2': _L1_ffn_in['rb2'], 'L1_ffn_sg': _L1_ffn_in['sg'], 'L1_ffn_sgb': _L1_ffn_in['sgb'], 'L1_ffn_sw1': _L1_ffn_in['sw1'], 'L1_ffn_sb1': _L1_ffn_in['sb1'], 'L1_ffn_sw2': _L1_ffn_in['sw2'], 'L1_ffn_sb2': _L1_ffn_in['sb2']}

def reference(x, itok_B_0_7, fside_8xS_0, itok_B_1_198, L0_cond_weights, L0_ffn_w1, L0_ffn_b1, L0_ffn_w2, L0_ffn_b2, L1_cond_weights, L1_ffn_wa, L1_ffn_rg, L1_ffn_rgb, L1_ffn_rw1, L1_ffn_rb1, L1_ffn_rw2, L1_ffn_rb2, L1_ffn_sg, L1_ffn_sgb, L1_ffn_sw1, L1_ffn_sb1, L1_ffn_sw2, L1_ffn_sb2):
    import jax
    import jax.numpy as jnp

    def _L0_cond_ref(x, subjects, weights, bias):
        import jax, jax.numpy as jnp
        import numpy as np
        B, C, T = (64, 32, 256)
        D, N = (32, 8)
        w = weights[subjects]
        b = bias[subjects]
        out = jnp.einsum('bct,bcd->bdt', x, w)
        out = out + b[:, :, None]
        return out

    def _L0_ffn_ref(x, w1, b1, w2, b2):
        import jax, jax.numpy as jnp
        import numpy as np
        DIM = 256
        INNER = 1024
        EPS_RMS = 1e-06
        EPS_Q = 1e-05

        def simple_rms_norm(x, dim):
            rms = jnp.sqrt(jnp.mean(x * x, axis=-1, keepdims=True) + EPS_RMS)
            return x / rms * dim ** (-0.5)

        def activation_quant(x):
            scale = 127.0 / jnp.clip(jnp.max(jnp.abs(x), axis=-1, keepdims=True), EPS_Q)
            return jnp.clip(jnp.round(x * scale), -128, 127) / scale

        def weight_quant(w):
            return jnp.sign(w) * jnp.mean(jnp.abs(w))

        def bit_linear(x, w, b, dim_in):
            x_norm = simple_rms_norm(x, dim_in)
            x_q = activation_quant(x_norm)
            w_q = weight_quant(w)
            return jnp.einsum('bsd,od->bso', x_q, w_q) + b
        h = bit_linear(x, w1, b1, DIM)
        h = jax.nn.gelu(h, approximate=False)
        return bit_linear(h, w2, b2, INNER)

    def _L1_cond_ref(x, conditions, weights):
        import jax, jax.numpy as jnp
        import numpy as np
        B, C, T = (128, 32, 256)
        S, D = (200, 32)
        w = weights[conditions]
        return jnp.einsum('bct,bcd->bdt', x, w)

    def _L1_ffn_ref(x, wa, rg, rgb, rw1, rb1, rw2, rb2, sg, sgb, sw1, sb1, sw2, sb2):
        import jax, jax.numpy as jnp
        import numpy as np
        B, S, D, F, E, SH, K = (2, 256, 256, 128, 16, 2, 2)

        def _experts_all(x, g, gb, w1, b1, w2, b2):
            y = jax.nn.gelu(jnp.einsum('bsd,edf->bsef', x, g) + gb, approximate=False)
            y = y * (jnp.einsum('bsd,edf->bsef', x, w1) + b1)
            return jnp.einsum('bsef,efd->bsed', y, w2) + b2
        aff = jax.nn.sigmoid(jnp.einsum('bsd,de->bse', x, wa))
        topk_p, topk_i = jax.lax.top_k(aff, K)
        topk_p = topk_p / jnp.sum(topk_p, axis=-1, keepdims=True)
        combine = jnp.sum(jax.nn.one_hot(topk_i, E, dtype=x.dtype) * topk_p[..., None], axis=2)
        routed = jnp.einsum('bsed,bse->bsd', _experts_all(x, rg, rgb, rw1, rb1, rw2, rb2), combine)
        shared = jnp.sum(_experts_all(x, sg, sgb, sw1, sb1, sw2, sb2), axis=2)
        return x + shared + routed
    x = x + _L0_ffn_ref(_L0_cond_ref(x, itok_B_0_7, L0_cond_weights, fside_8xS_0), L0_ffn_w1, L0_ffn_b1, L0_ffn_w2, L0_ffn_b2)
    x = x + _L1_ffn_ref(_L1_cond_ref(x, itok_B_1_198, L1_cond_weights), L1_ffn_wa, L1_ffn_rg, L1_ffn_rgb, L1_ffn_rw1, L1_ffn_rb1, L1_ffn_rw2, L1_ffn_rb2, L1_ffn_sg, L1_ffn_sgb, L1_ffn_sw1, L1_ffn_sb1, L1_ffn_sw2, L1_ffn_sb2)
    return x

_drawn_inputs = setup_inputs


def setup_inputs(seed=0):
    import zlib

    import numpy as np

    out = dict(_drawn_inputs(seed))
    spreads = {'L1_ffn_rgb': (0.0, 0.8),
     'L1_ffn_rb1': (0.0, 0.8),
     'L1_ffn_rb2': (0.0, 0.8),
     'L1_ffn_sgb': (0.0, 0.8),
     'L1_ffn_sb1': (0.0, 0.8),
     'L1_ffn_sb2': (0.0, 0.401)}
    factors = {'fside_8xS_0': 8.0,
     'L0_cond_weights': 4.769,
     'L0_ffn_w1': 4.741,
     'L0_ffn_b1': 4.694,
     'L0_ffn_w2': 3.471,
     'L0_ffn_b2': 3.033,
     'L1_ffn_rg': 8.0,
     'L1_ffn_rw1': 8.0,
     'L1_ffn_rw2': 8.0,
     'L1_ffn_sg': 4.314,
     'L1_ffn_sw1': 4.141,
     'L1_ffn_sw2': 4.016}
    for name, (base, spread) in spreads.items():
        noise = np.random.default_rng([zlib.crc32(name.encode()), seed]).standard_normal(out[name].shape)
        drawn = base * np.exp(spread * noise) if base else spread * noise
        out[name] = jnp.asarray(drawn.astype(out[name].dtype))
    for name, factor in factors.items():
        out[name] = (out[name] * factor).astype(out[name].dtype)
    return out
```

```python
import numpy as np
import concourse.bass as bass
from concourse import mybir
from contextlib import ExitStack

P = 128
B, C, D = 32, 32, 256
NT = B * C // P
BT = P // C
KD = D // P
F1 = 1024
KF = F1 // P
E, SH, TOPK = 16, 2, 2
F = 128
N0, N1 = 8, 200
EPS_RMS, EPS_Q, QMAX = 1e-6, 1e-5, 127.0
MAGIC = 1.5 * 2.0 ** 23
NS = (B * C * TOPK + E * (P - 1)) // P
RING = 4
WCOLS = 3 * D + 2
GO, UO, DO, GB, UB = 0, D, 2 * D, 3 * D, 3 * D + 1


def adaln_moe(nc, x, idx0, idx1, table0, table1, w1t, b1, w2t, b2, wa, wshared, wrouted, bdown, out):
    f32, bf16, i32, u32 = mybir.dt.float32, mybir.dt.bfloat16, mybir.dt.int32, mybir.dt.uint32
    ALU, ACT, AX = mybir.AluOpType, mybir.ActivationFunctionType, mybir.AxisListType

    ctx = ExitStack()
    with ctx:
        def sb(name, shape, dt=f32):
            return ctx.enter_context(nc.sbuf_tensor(name, shape, dt))

        def ps(name, shape, dt=f32):
            return ctx.enter_context(nc.psum_tensor(name, shape, dt))

        def sem(name):
            return ctx.enter_context(nc.semaphore(name))

        def sems(name, n):
            return [sem(f"{name}{i}") for i in range(n)]

        slot_in = nc.dram_tensor("slot_in", [NS * P, D], f32).ap()
        slot_out = nc.dram_tensor("slot_out", [NS * P, D], f32).ap()

        idx_sb = sb("idx_sb", [P, 2, B], i32)
        pidx = sb("pidx", [P, 1], i32)
        cidx = sb("cidx", [P, 1], i32)
        rowidx = sb("rowidx", [P, 2, NT], i32)
        cond0 = sb("cond0", [P, NT, C + 1])
        cond1 = sb("cond1", [P, NT, C])
        blk0 = sb("blk0", [P, NT, P])
        blk1 = sb("blk1", [P, NT, P])
        blkmask = sb("blkmask", [P, BT])
        x_sb = sb("x_sb", [P, NT, D])
        xb_sb = sb("xb_sb", [P, NT, D])
        x1_sb = sb("x1_sb", [P, NT, D])
        y_sb = sb("y_sb", [P, NT, D])
        yT_sb = sb("yT_sb", [P, KD, NT, P])
        w1_sb = sb("w1_sb", [P, KD, F1])
        w2_sb = sb("w2_sb", [P, KF, D])
        w1s = sb("w1s", [P, KD, F1], bf16)
        w2s = sb("w2s", [P, KF, D], bf16)
        wabs = sb("wabs", [P, 2])
        wmean = sb("wmean", [P, 2])
        b1_sb = sb("b1_sb", [P, F1])
        b2_sb = sb("b2_sb", [P, D])
        wa_sb = sb("wa_sb", [P, KD, E])
        bdown_sb = sb("bdown_sb", [E + SH, D])
        ones_f = sb("ones_f", [P, P])
        ones_b = sb("ones_b", [P, P], bf16)
        before_b = sb("before_b", [P, P], bf16)
        ident_f = sb("ident_f", [P, P])
        ident_b = sb("ident_b", [P, P], bf16)
        zeros = sb("zeros", [P, 1, D])
        h0 = sb("h0", [P, NT, D])
        junk = sb("junk", [P, F1])
        st = [sb(f"stats{n}", [P, 8, NT]) for n in range(2)]
        halfneg = sb("halfneg", [P, NT])
        rq = sb("rq", [P, 2, F1])
        q = sb("q", [P, 2, F1], bf16)
        qT = sb("qT", [P, 2, KF, P], bf16)
        pre = sb("pre", [P, 2, F1])
        hid = sb("hid", [P, NT, F1])
        aff = sb("aff", [P, NT, E])
        top = sb("top", [P, NT, 8])
        topi = sb("topi", [P, NT, 8], u32)
        topf = sb("topf", [P, NT, TOPK])
        prob = sb("prob", [P, NT, TOPK])
        psum2 = sb("psum2", [P, NT])
        oneh = sb("oneh", [P, NT, TOPK, E])
        onep = sb("onep", [P, NT, TOPK, E])
        chosen = sb("chosen", [P, NT, E], bf16)
        comb = sb("comb", [P, NT, E + SH])
        combT = sb("combT", [E + SH, NT, P])
        eidx = sb("eidx", [P, E])
        full = sb("full", [P, NT])
        tidx = sb("tidx", [P, NS])
        lower = sb("lower", [P, E, E])
        more = sb("more", [P, E, NT])
        ntile = sb("ntile", [P, E])
        prior = sb("prior", [P, E, E])
        first = sb("first", [P, E])
        endt = sb("endt", [P, E])
        firsts = sb("firsts", [P, E])
        place = sb("place", [P, NT, E])
        placed = sb("placed", [P, NT, TOPK, E])
        slotf = sb("slotf", [P, NT, TOPK])
        slot = sb("slot", [P, NT, TOPK], i32)
        past = sb("past", [P, NS, E])
        texf = sb("texf", [P, NS])
        tex = sb("tex", [P, NS], i32)
        wsh = sb("wsh", [P, SH, WCOLS])
        shg = sb("shg", [P, 2, 4 * P])
        shy = w1_sb
        base = sb("base", [P, NT, D])
        wr = sb("wr", [P, RING, WCOLS])
        xr = x_sb[:, 0:RING, :]
        xrT = sb("xrT", [P, 2, KD, P])
        gl = sb("gl", [P, 2, P])
        yr = sb("yr", [P, 2, P])
        rr = x_sb[:, RING:2 * RING, :]
        picked = hid
        res = h0

        SS, AMAX, VAR, RINV, LIM, INV, SCALE, DEQ = range(8)

        S = [ps(f"S{i}", [P, 512]) for i in range(2)]
        T = [ps(f"T{i}", [P, 512]) for i in range(2)]
        M = [ps(f"M{i}", [P, 1024]) for i in range(2)]

        def T_b(i):
            return T[i][:, :].bitcast(bf16).rearrange("p (k m) -> p k m", m=P)

        def T_f(i):
            return T[i][:, 0:KD * P].rearrange("p (k m) -> p k m", m=P)

        d_idx, d_x, d_w1, d_w2, d_b, d_bx, d_wa, d_wsh, d_zero = (sem(n) for n in (
            "d_idx", "d_x", "d_w1", "d_w2", "d_b", "d_bx", "d_wa", "d_wsh", "d_zero"))
        d_cond0 = sems("d_cond0_", NT)
        d_cond1, d_scatter, d_rows, d_out = (sem(n) for n in ("d_cond1", "d_scatter", "d_rows", "d_out"))
        d_wr, d_xr, d_rr = sems("d_wr", RING), sems("d_xr", RING), sems("d_rr", RING)
        d_pick = sems("d_pick", NT)
        p_const, p_pow, p_blk1, p_xb, p_own = (sem(n) for n in ("p_const", "p_pow", "p_blk1", "p_xb", "p_own"))
        v_own, v_zero, v_row, v_blk0, v_abs, v_mean, v_max0, v_var, v_scale, v_q0, v_qT0, v_pre = (sem(n) for n in (
            "v_own", "v_zero", "v_row", "v_blk0", "v_abs", "v_mean", "v_max0", "v_var", "v_scale", "v_q0", "v_qT0", "v_pre"))
        v_max1, v_q1, v_qT1, v_x1, v_yT, v_chosen, v_comb, v_slot, v_tex, v_combT = (sem(n) for n in (
            "v_max1", "v_q1", "v_qT1", "v_x1", "v_yT", "v_chosen", "v_comb", "v_slot", "v_tex", "v_combT"))
        v_shy, v_base, v_xrT, v_yr, v_res = (sem(n) for n in ("v_shy", "v_base", "v_xrT", "v_yr", "v_res"))
        a_sign, a_h0, a_sq0, a_rq0, a_gelu, a_sq1, a_rq1, a_y, a_aff, a_shg, a_gl, a_rr = (sem(n) for n in (
            "a_sign", "a_h0", "a_sq0", "a_rq0", "a_gelu", "a_sq1", "a_rq1", "a_y", "a_aff", "a_shg", "a_gl", "a_rr"))
        t_mean, t_c0, t_qT0, t_mm1, t_qT1, t_mm2, t_c1, t_yT, t_logit, t_rank, t_tot, t_combT = (sem(n) for n in (
            "t_mean", "t_c0", "t_qT0", "t_mm1", "t_qT1", "t_mm2", "t_c1", "t_yT", "t_logit", "t_rank", "t_tot", "t_combT"))
        t_sh, t_base, t_xr, t_gu, t_dn = (sem(n) for n in ("t_sh", "t_base", "t_xr", "t_gu", "t_dn"))

        HALF = NT // 2
        LAG_Q1, LAG_X1, LAG_Y = 6, 7, 8
        STEPS = NT + LAG_Y + 1

        def at(i, lag):
            return i - lag if 0 <= i - lag < NT else None

        block = ctx.enter_context(nc.Block())

        @block.sync
        def _(sp):
            sp.dma_start(idx_sb[:, 0, :], idx0.partition_broadcast(P)).then_inc(d_idx, 16)
            sp.dma_start(idx_sb[:, 1, :], idx1.partition_broadcast(P)).then_inc(d_idx, 16)
            sp.dma_start(w1_sb[:, :, :], w1t.rearrange("(k p) o -> p k o", p=P)).then_inc(d_w1, 16)
            sp.dma_start(w2_sb[:, :, :], w2t.rearrange("(k p) o -> p k o", p=P)).then_inc(d_w2, 16)
            sp.dma_start(b1_sb[:, :], b1.partition_broadcast(P)).then_inc(d_b, 16)
            sp.dma_start(wa_sb[:, :, :], wa.rearrange("(k p) e -> p k e", p=P)).then_inc(d_wa, 16)
            sp.dma_start(bdown_sb[:, :], bdown).then_inc(d_wa, 16)
            for e in range(SH):
                sp.dma_start(wsh[:, e, :], wshared[e]).then_inc(d_wsh, 16)
            sp.wait_ge(v_zero, 1)
            sp.dma_start(slot_in.rearrange("(t p) d -> p t d", p=P),
                         zeros[:, :, :].to_broadcast([P, NS, D])).then_inc(d_zero, 16)

            def load(t, s, n):
                if n:
                    sp.wait_ge(t_dn, t - RING + 1)
                e = sp.value_load(tex[0:1, bass.ds(t, 1)], min_val=0, max_val=E - 1)
                sp.dma_start(wr[:, s, :], wrouted[bass.ds(e, 1)].rearrange("a p n -> p (a n)")).then_inc(d_wr[s], 16)
                sp.dma_start(xr[:, s, :], slot_in[bass.ds(t * P, P), :]).then_inc(d_xr[s], 16)

            def store(t, s):
                sp.wait_ge(a_rr, t + 1)
                sp.dma_start(slot_out[bass.ds(t * P, P), :], rr[:, s, :]).then_inc(d_rr[s], 16)

            sp.wait_ge(v_tex, 1)
            sp.wait_ge(d_scatter, 16 * NT * TOPK)
            for t in range(NS):
                load(t, t % RING, t // RING)
                if t >= RING - 1:
                    store(t - RING + 1, (t - RING + 1) % RING)
            for t in range(NS - RING + 1, NS):
                store(t, t % RING)
            for g in range(NT):
                sp.wait_ge(v_res, g + 1)
                sp.dma_start(out[g * P:(g + 1) * P, :], res[:, g, :]).then_inc(d_out, 16)
            sp.wait_ge(d_out, 16 * NT)

        @block.gpsimd
        def _(pool):
            nc.gpsimd.iota(pidx[:, :], [[0, 1]], base=0, channel_multiplier=1).then_inc(p_const, 1)
            nc.gpsimd.memset(blkmask[:, :], 1.0).then_inc(p_own, 1)
            pool.wait_ge(p_own, 1)
            nc.gpsimd.affine_select(out=blkmask[:, :], in_=blkmask[:, :], pattern=[[-C, BT]], compare_op=ALU.is_ge,
                                    fill=0.0, base=0, channel_multiplier=1).then_inc(p_own, 1)
            pool.wait_ge(p_own, 2)
            nc.gpsimd.affine_select(out=blkmask[:, :], in_=blkmask[:, :], pattern=[[C, BT]], compare_op=ALU.is_ge,
                                    fill=0.0, base=C - 1, channel_multiplier=-1).then_inc(p_const, 1)
            pool.wait_ge(v_row, 1)
            for g in range(NT):
                nc.gpsimd.indirect_dma_start(cond0[:, g, :], None, table0,
                                             bass.IndirectOffsetOnAxis(ap=rowidx[:, 0, g:g + 1], axis=0)).then_inc(d_cond0[g], 16)
            own = 2

            def made(ins):
                nonlocal own
                own += 1
                ins.then_inc(p_own, 1)
                pool.wait_ge(p_own, own)

            for m in (ident_b, ident_f):
                made(nc.gpsimd.memset(m[:, :], 0.0))
                nc.gpsimd.affine_select(out=m[:, :], in_=m[:, :], pattern=[[-1, P]], compare_op=ALU.not_equal,
                                        fill=1.0, base=0, channel_multiplier=1).then_inc(p_const, 1)
            nc.gpsimd.memset(halfneg[:, :], -0.5).then_inc(p_const, 1)
            for g in range(NT):
                nc.gpsimd.indirect_dma_start(cond1[:, g, :], None, table1,
                                             bass.IndirectOffsetOnAxis(ap=rowidx[:, 1, g:g + 1], axis=0)).then_inc(d_cond1, 16)
            made(nc.gpsimd.memset(before_b[:, :], 0.0))
            nc.gpsimd.affine_select(out=before_b[:, :], in_=before_b[:, :], pattern=[[-1, P]], compare_op=ALU.is_ge,
                                    fill=1.0, base=0, channel_multiplier=1).then_inc(p_const, 1)
            made(nc.gpsimd.memset(lower[:, :, :], 0.0))
            nc.gpsimd.affine_select(out=lower[:, :, :], in_=lower[:, :, :], pattern=[[-1, E], [1, E]], compare_op=ALU.is_ge,
                                    fill=1.0, base=0, channel_multiplier=0).then_inc(p_const, 1)
            nc.gpsimd.iota(eidx[:, :], [[1, E]], base=0, channel_multiplier=0,
                           allow_small_or_imprecise_dtypes=True).then_inc(p_const, 1)
            nc.gpsimd.iota(tidx[:, :], [[1, NS]], base=0, channel_multiplier=0,
                           allow_small_or_imprecise_dtypes=True).then_inc(p_const, 1)
            nc.gpsimd.iota(full[:, :], [[P, NT]], base=0, channel_multiplier=0,
                           allow_small_or_imprecise_dtypes=True).then_inc(p_const, 1)
            nc.gpsimd.memset(comb[:, :, E:E + SH], 1.0).then_inc(p_const, 1)

            def inverse_root(layer, half):
                c = slice(half * HALF, (half + 1) * HALF)
                pool.wait_ge(v_var, 2 * layer + half + 1)
                nc.gpsimd.tensor_tensor(st[layer][:, RINV, c], st[layer][:, VAR, c], halfneg[:, c], ALU.pow).then_inc(p_pow, 1)

            inverse_root(0, 0)
            inverse_root(0, 1)
            pool.wait_ge(d_cond1, 16 * NT)
            for g in range(NT):
                nc.gpsimd.tensor_tensor(blk1[:, g, :].rearrange("p (q c) -> p q c", q=BT),
                                        cond1[:, g, :].unsqueeze(1).to_broadcast([P, BT, C]),
                                        blkmask[:, :].unsqueeze(2).to_broadcast([P, BT, C]), ALU.mult).then_inc(p_blk1, 1)
            pool.wait_ge(d_x, 32)
            pool.wait_ge(d_bx, 16)
            for g in range(NT):
                nc.gpsimd.tensor_tensor(xb_sb[:, g, :], x_sb[:, g, :], b2_sb[:, :], ALU.add).then_inc(p_xb, 1)
            inverse_root(1, 0)
            inverse_root(1, 1)

            pool.wait_ge(v_slot, 1)
            pool.wait_ge(a_y, NT)
            pool.wait_ge(d_zero, 16)
            for g in range(NT):
                for k in range(TOPK):
                    nc.gpsimd.indirect_dma_start(slot_in, bass.IndirectOffsetOnAxis(ap=slot[:, g, k:k + 1], axis=0),
                                                 y_sb[:, g, :], None).then_inc(d_scatter, 16)
            for s in range(RING):
                pool.wait_ge(d_rr[s], 16 * len(range(s, NS, RING)))
            for g in range(NT):
                for k in range(TOPK):
                    nc.gpsimd.indirect_dma_start(picked[:, g, k * D:(k + 1) * D], None, slot_out,
                                                 bass.IndirectOffsetOnAxis(ap=slot[:, g, k:k + 1], axis=0)).then_inc(d_pick[g], 16)

        @block.scalar
        def _(act):
            act.dma_start(x_sb[:, 0:HALF, :], x[0:HALF * P].rearrange("(g p) d -> p g d", p=P)).then_inc(d_x, 16)
            act.dma_start(x_sb[:, HALF:NT, :], x[HALF * P:].rearrange("(g p) d -> p g d", p=P)).then_inc(d_x, 16)
            act.dma_start(b2_sb[:, :], b2.partition_broadcast(P)).then_inc(d_bx, 16)
            act.wait_ge(d_w1, 16)
            nc.scalar.activation(w1s[:, :, :], w1_sb[:, :, :], ACT.Sign).then_inc(a_sign, 1)
            act.wait_ge(d_w2, 16)
            nc.scalar.activation(w2s[:, :, :], w2_sb[:, :, :], ACT.Sign).then_inc(a_sign, 1)
            for g in range(NT):
                act.wait_ge(t_c0, g + 1)
                act.wait_ge(d_cond0[g], 16)
                nc.scalar.activation(h0[:, g, :], S[g % 2][:, 0:D], ACT.Identity, bias=cond0[:, g, C:C + 1]).then_inc(a_h0, 1)
                act.wait_ge(a_h0, g + 1)
                nc.scalar.activation(junk[:, 0:D], h0[:, g, :], ACT.Square, accum_out=st[0][:, SS, g:g + 1]).then_inc(a_sq0, 1)
            for i in range(STEPS):
                if (g := at(i, 0)) is not None:
                    act.wait_ge(v_scale, g // HALF + 1)
                    if g >= 2:
                        act.wait_ge(v_q0, g - 1)
                    nc.scalar.activation(rq[:, g % 2, 0:D], h0[:, g, :], ACT.Copy, bias=MAGIC,
                                         scale=st[0][:, SCALE, g:g + 1]).then_inc(a_rq0, 1)
                if (g := at(i, 1)) is not None:
                    act.wait_ge(v_pre, g + 1)
                    nc.scalar.activation(hid[:, g, :], pre[:, g % 2, :], ACT.Gelu).then_inc(a_gelu, 1)
                    act.wait_ge(a_gelu, g + 1)
                    nc.scalar.activation(junk[:, :], hid[:, g, :], ACT.Square, accum_out=st[1][:, SS, g:g + 1]).then_inc(a_sq1, 1)
                if (g := at(i, LAG_Q1)) is not None:
                    act.wait_ge(v_scale, g // HALF + 3)
                    act.wait_ge(v_q0, min(g + LAG_Q1, NT))
                    if g >= 2:
                        act.wait_ge(v_q1, g - 1)
                    nc.scalar.activation(rq[:, g % 2, :], hid[:, g, :], ACT.Copy, bias=MAGIC,
                                         scale=st[1][:, SCALE, g:g + 1]).then_inc(a_rq1, 1)
                if (g := at(i, LAG_Y)) is not None:
                    act.wait_ge(t_c1, g + 1)
                    nc.scalar.activation(y_sb[:, g, :], S[1][:, 0:D], ACT.Copy).then_inc(a_y, 1)
            act.wait_ge(t_logit, NT)
            nc.scalar.activation(aff[:, :, :], M[0][:, 0:NT * E].rearrange("p (g e) -> p g e", e=E), ACT.Sigmoid).then_inc(a_aff, 1)
            act.wait_ge(d_wsh, 16 * SH)
            for n in range(2 * SH):
                act.wait_ge(t_sh, n + 1)
                if n >= 2:
                    act.wait_ge(v_shy, n - 1)
                nc.scalar.activation(shg[:, n % 2, :], M[n % 2][:, 0:4 * P], ACT.Gelu,
                                     bias=wsh[:, n % SH, GB:GB + 1]).then_inc(a_shg, 1)

            def gate(t, s, n):
                act.wait_ge(t_gu, t + 1)
                act.wait_ge(d_wr[s], 16 * (n + 1))
                act.wait_ge(v_yr, t - 1) if n or s >= 2 else None
                nc.scalar.activation(gl[:, s % 2, :], M[s % 2][:, 0:P], ACT.Gelu, bias=wr[:, s, GB:GB + 1]).then_inc(a_gl, 1)

            def rows(t, s, n):
                act.wait_ge(t_dn, t + 1)
                if n:
                    act.wait_ge(d_rr[s], 16 * n)
                nc.scalar.activation(rr[:, s, :], S[s % 2][:, 0:D], ACT.Copy).then_inc(a_rr, 1)

            for t in range(NS):
                gate(t, t % RING, t // RING)
                if t:
                    rows(t - 1, (t - 1) % RING, (t - 1) // RING)
            rows(NS - 1, (NS - 1) % RING, (NS - 1) // RING)

        @block.vector
        def _(dve):
            own = 0

            def then(ins):
                nonlocal own
                own += 1
                ins.then_inc(v_own, 1)
                dve.wait_ge(v_own, own)

            dve.wait_ge(p_const, 1)
            then(nc.vector.tensor_scalar(cidx[:, :], pidx[:, :], C - 1, None, ALU.bitwise_and))
            dve.wait_ge(d_idx, 32)
            for b in range(BT):
                r = slice(b * C, (b + 1) * C)
                last = nc.vector.tensor_scalar(rowidx[r, :, :], idx_sb[r, :, :].rearrange("p l (g b) -> p l g b", b=BT)[:, :, :, b],
                                               float(C), cidx[r, :], ALU.mult, ALU.add)
            last.then_inc(v_row, 1)
            nc.vector.memset(zeros[:, :, :], 0.0).then_inc(v_zero, 1)
            nc.vector.memset(ones_b[:, :], 1.0)
            nc.vector.memset(ones_f[:, :], 1.0).then_inc(v_zero, 1)
            for n, (w, d) in enumerate(((w1_sb, d_w1), (w2_sb, d_w2))):
                dve.wait_ge(d, 16)
                nc.vector.tensor_reduce(wabs[:, n:n + 1], w[:, :, :], AX.XY, ALU.add, apply_absolute_value=True).then_inc(v_abs, 1)
            dve.wait_ge(p_const, 2)
            for g in range(NT):
                dve.wait_ge(d_cond0[g], 16)
                nc.vector.tensor_tensor(blk0[:, g, :].rearrange("p (q c) -> p q c", q=BT),
                                        cond0[:, g, 0:C].unsqueeze(1).to_broadcast([P, BT, C]),
                                        blkmask[:, :].unsqueeze(2).to_broadcast([P, BT, C]), ALU.mult).then_inc(v_blk0, 1)
            dve.wait_ge(t_mean, 1)
            nc.vector.tensor_scalar(wmean[:, :], T[1][:, 0:2], 1.0 / (D * F1), None, ALU.mult).then_inc(v_mean, 1)
            dve.wait_ge(v_mean, 1)

            def scales(layer, half, width):
                c = slice(half * HALF, (half + 1) * HALF)
                s = st[layer]
                dve.wait_ge((a_sq0, a_sq1)[layer], (half + 1) * HALF)
                nc.vector.tensor_scalar(s[:, VAR, c], s[:, SS, c], 1.0 / width, EPS_RMS, ALU.mult, ALU.add).then_inc(v_var, 1)
                dve.wait_ge(p_pow, 2 * layer + half + 1)
                dve.wait_ge((v_max0, v_max1)[layer], (half + 1) * HALF)
                then(nc.vector.tensor_tensor(s[:, LIM, c], s[:, AMAX, c], s[:, RINV, c], ALU.mult))
                then(nc.vector.tensor_scalar(s[:, LIM, c], s[:, LIM, c], width ** -0.5, EPS_Q, ALU.mult, ALU.max))
                then(nc.vector.reciprocal(s[:, INV, c], s[:, LIM, c]))
                then(nc.vector.tensor_scalar(s[:, INV, c], s[:, INV, c], QMAX * width ** -0.5, None, ALU.mult))
                nc.vector.tensor_tensor(s[:, SCALE, c], s[:, INV, c], s[:, RINV, c], ALU.mult).then_inc(v_scale, 1)
                then(nc.vector.tensor_scalar(s[:, DEQ, c], s[:, LIM, c], wmean[:, layer:layer + 1], 1.0 / QMAX, ALU.mult, ALU.mult))

            for half in range(2):
                for g in range(half * HALF, (half + 1) * HALF):
                    dve.wait_ge(a_h0, g + 1)
                    nc.vector.tensor_reduce(st[0][:, AMAX, g:g + 1], h0[:, g, :], AX.X, ALU.max, apply_absolute_value=True).then_inc(v_max0, 1)
                scales(0, half, D)

            dve.wait_ge(d_b, 16)
            for i in range(STEPS):
                if (g := at(i, 0)) is not None:
                    dve.wait_ge(a_rq0, g + 1)
                    if g >= 2:
                        dve.wait_ge(t_qT0, g - 1)
                    nc.vector.tensor_scalar(q[:, g % 2, 0:D], rq[:, g % 2, 0:D], -MAGIC, None, ALU.add).then_inc(v_q0, 1)
                    dve.wait_ge(t_qT0, g + 1)
                    if g >= 2:
                        dve.wait_ge(t_mm1, g - 1)
                    nc.vector.tensor_copy(qT[:, g % 2, 0:KD, :], T_b(0)[:, 0:KD, :]).then_inc(v_qT0, 1)
                if (g := at(i, 1)) is not None:
                    dve.wait_ge(t_mm1, g + 1)
                    if g >= 2:
                        dve.wait_ge(a_gelu, g - 1)
                    nc.vector.scalar_tensor_tensor(pre[:, g % 2, :], M[g % 2][:, :], st[0][:, DEQ, g:g + 1], b1_sb[:, :],
                                                   ALU.mult, ALU.add).then_inc(v_pre, 1)
                if (g := at(i, 2)) is not None:
                    dve.wait_ge(a_gelu, g + 1)
                    nc.vector.tensor_reduce(st[1][:, AMAX, g:g + 1], hid[:, g, :], AX.X, ALU.max, apply_absolute_value=True).then_inc(v_max1, 1)
                    if g % HALF == HALF - 1:
                        scales(1, g // HALF, F1)
                if (g := at(i, LAG_Q1)) is not None:
                    dve.wait_ge(a_rq1, g + 1)
                    dve.wait_ge(t_qT0, min(g + LAG_Q1, NT))
                    if g >= 2:
                        dve.wait_ge(t_qT1, g - 1)
                    nc.vector.tensor_scalar(q[:, g % 2, :], rq[:, g % 2, :], -MAGIC, None, ALU.add).then_inc(v_q1, 1)
                    dve.wait_ge(t_qT1, g + 1)
                    dve.wait_ge(t_mm1, min(g + LAG_Q1, NT))
                    if g >= 2:
                        dve.wait_ge(t_mm2, g - 1)
                    nc.vector.tensor_copy(qT[:, g % 2, :, :], T_b(1)).then_inc(v_qT1, 1)
                if (g := at(i, LAG_X1)) is not None:
                    dve.wait_ge(t_mm2, g + 1)
                    dve.wait_ge(p_xb, g + 1)
                    nc.vector.scalar_tensor_tensor(x1_sb[:, g, :], S[0][:, 0:D], st[1][:, DEQ, g:g + 1], xb_sb[:, g, :],
                                                   ALU.mult, ALU.add).then_inc(v_x1, 1)
                if (g := at(i, LAG_Y)) is not None:
                    dve.wait_ge(t_yT, g + 1)
                    nc.vector.tensor_copy(yT_sb[:, :, g, :], T_f(0)).then_inc(v_yT, 1)

            dve.wait_ge(a_aff, 1)
            for g in range(NT):
                last = nc.vector.max(top[:, g, :], aff[:, g, :])
            then(last)
            for g in range(NT):
                last = nc.vector.max_index(topi[:, g, :], top[:, g, :], aff[:, g, :])
            then(last)
            then(nc.vector.tensor_copy(topf[:, :, :], topi[:, :, 0:TOPK]))
            dve.wait_ge(p_const, 10)
            then(nc.vector.tensor_tensor(oneh[:, :, :, :], topf[:, :, :].unsqueeze(3).to_broadcast([P, NT, TOPK, E]),
                                         eidx[:, :].unsqueeze(1).unsqueeze(1).to_broadcast([P, NT, TOPK, E]), ALU.is_equal))
            nc.vector.tensor_tensor(chosen[:, :, :], oneh[:, :, 0, :], oneh[:, :, 1, :], ALU.add).then_inc(v_chosen, 1)
            then(nc.vector.tensor_tensor(psum2[:, :], top[:, :, 0], top[:, :, 1], ALU.add))
            then(nc.vector.reciprocal(psum2[:, :], psum2[:, :]))
            then(nc.vector.tensor_tensor(prob[:, :, :], top[:, :, 0:TOPK], psum2[:, :].unsqueeze(2).to_broadcast([P, NT, TOPK]), ALU.mult))
            then(nc.vector.tensor_tensor(onep[:, :, :, :], oneh[:, :, :, :], prob[:, :, :].unsqueeze(3).to_broadcast([P, NT, TOPK, E]), ALU.mult))
            nc.vector.tensor_tensor(comb[:, :, 0:E], onep[:, :, 0, :], onep[:, :, 1, :], ALU.add).then_inc(v_comb, 1)
            dve.wait_ge(t_tot, 1)
            then(nc.vector.tensor_tensor(more[:, :, :], T[1][:, P:P + E].unsqueeze(2).to_broadcast([P, E, NT]),
                                         full[:, :].unsqueeze(1).to_broadcast([P, E, NT]), ALU.is_gt))
            then(nc.vector.tensor_reduce(ntile[:, :], more[:, :, :], AX.X, ALU.add))
            then(nc.vector.tensor_tensor(prior[:, :, :], ntile[:, :].unsqueeze(1).to_broadcast([P, E, E]), lower[:, :, :], ALU.mult))
            then(nc.vector.tensor_reduce(first[:, :], prior[:, :, :], AX.X, ALU.add))
            then(nc.vector.tensor_scalar(firsts[:, :], first[:, :], float(P), None, ALU.mult))
            then(nc.vector.tensor_tensor(place[:, :, :], T[1][:, 0:NT * E].rearrange("p (g e) -> p g e", e=E),
                                         firsts[:, :].unsqueeze(1).to_broadcast([P, NT, E]), ALU.add))
            then(nc.vector.tensor_tensor(placed[:, :, :, :], oneh[:, :, :, :],
                                         place[:, :, :].unsqueeze(2).to_broadcast([P, NT, TOPK, E]), ALU.mult))
            then(nc.vector.tensor_reduce(slotf[:, :, :], placed[:, :, :, :], AX.X, ALU.add))
            nc.vector.tensor_copy(slot[:, :, :], slotf[:, :, :]).then_inc(v_slot, 1)
            then(nc.vector.tensor_tensor(endt[:, :], first[:, :], ntile[:, :], ALU.add))
            then(nc.vector.tensor_tensor(past[:, :, :], endt[:, :].unsqueeze(1).to_broadcast([P, NS, E]),
                                         tidx[:, :].unsqueeze(2).to_broadcast([P, NS, E]), ALU.is_le))
            then(nc.vector.tensor_reduce(texf[:, :], past[:, :, :], AX.X, ALU.add))
            nc.vector.tensor_scalar(tex[:, :], texf[:, :], E - 1.0, None, ALU.min).then_inc(v_tex, 1)

            for h in range(2):
                dve.wait_ge(t_combT, h + 1)
                nc.vector.tensor_copy(combT[:, h * 4:(h + 1) * 4, :], T[0][0:E + SH, :].rearrange("p (g m) -> p g m", m=P)).then_inc(v_combT, 1)
            for n in range(2 * SH):
                dve.wait_ge(a_shg, n + 1)
                nc.vector.scalar_tensor_tensor(shy[:, n % SH, (n // SH) * 4 * P:(n // SH + 1) * 4 * P], M[n % 2][:, 4 * P:8 * P],
                                               wsh[:, n % SH, UB:UB + 1], shg[:, n % 2, :], ALU.add, ALU.mult).then_inc(v_shy, 1)
            for g in range(NT):
                then(nc.vector.tensor_tensor(base[:, g, :], x1_sb[:, g, :], y_sb[:, g, :], ALU.add))
                dve.wait_ge(t_base, g + 1)
                nc.vector.tensor_tensor(base[:, g, :], base[:, g, :], S[g % 2][:, 0:D], ALU.add).then_inc(v_base, 1)

            def turned(t, s):
                dve.wait_ge(t_xr, t + 1)
                if not (isinstance(t, int) and t < 2):
                    dve.wait_ge(t_gu, t - 1)
                nc.vector.tensor_copy(xrT[:, s % 2, :, :], T_f(s % 2)).then_inc(v_xrT, 1)

            def gated(t, s):
                dve.wait_ge(a_gl, t + 1)
                if not (isinstance(t, int) and t < 2):
                    dve.wait_ge(t_dn, t - 1)
                nc.vector.scalar_tensor_tensor(yr[:, s % 2, :], M[s % 2][:, P:2 * P], wr[:, s, UB:UB + 1], gl[:, s % 2, :],
                                               ALU.add, ALU.mult).then_inc(v_yr, 1)

            turned(0, 0)
            for t in range(NS):
                if t + 1 < NS:
                    turned(t + 1, (t + 1) % RING)
                gated(t, t % RING)
            for g in range(NT):
                dve.wait_ge(d_pick[g], 32)
                then(nc.vector.scalar_tensor_tensor(base[:, g, :], picked[:, g, 0:D], prob[:, g, 0:1], base[:, g, :], ALU.mult, ALU.add))
                nc.vector.scalar_tensor_tensor(res[:, g, :], picked[:, g, D:2 * D], prob[:, g, 1:2], base[:, g, :],
                                               ALU.mult, ALU.add).then_inc(v_res, 1)

        @block.tensor
        def _(pe):
            def mm(o, l, r, start=True, stop=True):
                return nc.tensor.matmul(o, l, r, start=start, stop=stop)

            pe.wait_ge(v_zero, 2)
            pe.wait_ge(v_abs, 2)
            mm(T[1][:, 0:2], ones_f[:, :], wabs[:, :]).then_inc(t_mean, 1)
            for g in range(NT):
                pe.wait_ge(v_blk0, g + 1)
                pe.wait_ge(d_x, 32)
                if g >= 2:
                    pe.wait_ge(a_h0, g - 1)
                mm(S[g % 2][:, 0:D], blk0[:, g, :], x_sb[:, g, :]).then_inc(t_c0, 1)
            pe.wait_ge(p_const, 4)
            pe.wait_ge(a_sign, 2)
            for i in range(STEPS + 1):
                if (g := at(i, 0)) is not None:
                    pe.wait_ge(v_q0, g + 1)
                    if g:
                        pe.wait_ge(v_qT0, g)
                    for k in range(KD):
                        last = nc.tensor.transpose(T_b(0)[:, k, :], q[:, g % 2, k * P:(k + 1) * P], ident_b[:, :])
                    last.then_inc(t_qT0, 1)
                    pe.wait_ge(v_qT0, g + 1)
                    if g >= 2:
                        pe.wait_ge(v_pre, g - 1)
                    for n in range(2):
                        for k in range(KD):
                            last = mm(M[g % 2][:, n * 512:(n + 1) * 512], qT[:, g % 2, k, :], w1s[:, k, n * 512:(n + 1) * 512],
                                      k == 0, k == KD - 1)
                    last.then_inc(t_mm1, 1)
                if (g := at(i, LAG_Q1)) is not None:
                    pe.wait_ge(v_q1, g + 1)
                    pe.wait_ge(v_mean, 1)
                    if g:
                        pe.wait_ge(v_qT1, g)
                    for k in range(KF):
                        last = nc.tensor.transpose(T_b(1)[:, k, :], q[:, g % 2, k * P:(k + 1) * P], ident_b[:, :])
                    last.then_inc(t_qT1, 1)
                    pe.wait_ge(v_qT1, g + 1)
                    pe.wait_ge(a_h0, NT)
                    if g:
                        pe.wait_ge(v_x1, g)
                    for k in range(KF):
                        last = mm(S[0][:, 0:D], qT[:, g % 2, k, :], w2s[:, k, :], k == 0, k == KF - 1)
                    last.then_inc(t_mm2, 1)
                if (g := at(i, LAG_X1)) is not None:
                    pe.wait_ge(v_x1, g + 1)
                    pe.wait_ge(p_blk1, g + 1)
                    if g:
                        pe.wait_ge(a_y, g)
                    mm(S[1][:, 0:D], blk1[:, g, :], x1_sb[:, g, :]).then_inc(t_c1, 1)
                if (g := at(i, LAG_Y)) is not None:
                    pe.wait_ge(a_y, g + 1)
                    pe.wait_ge(v_qT0, NT)
                    if g:
                        pe.wait_ge(v_yT, g)
                    for k in range(KD):
                        last = nc.tensor.transpose(T_f(0)[:, k, :], y_sb[:, g, k * P:(k + 1) * P], ident_f[:, :])
                    last.then_inc(t_yT, 1)
                if (g := at(i, LAG_Y + 1)) is not None:
                    pe.wait_ge(v_yT, g + 1)
                    pe.wait_ge(v_pre, NT)
                    pe.wait_ge(d_wa, 32)
                    for k in range(KD):
                        last = mm(M[0][:, g * E:(g + 1) * E], yT_sb[:, k, g, :], wa_sb[:, k, :], k == 0, k == KD - 1)
                    last.then_inc(t_logit, 1)

            pe.wait_ge(d_wsh, 16 * SH)

            def shared(n):
                e, h = n % SH, n // SH
                if n >= 2:
                    pe.wait_ge(v_shy, n - 1)
                else:
                    pe.wait_ge(a_aff, 1)
                for o, c in ((0, GO), (4 * P, UO)):
                    for k in range(KD):
                        last = mm(M[n % 2][:, o:o + 4 * P], wsh[:, e, c + k * P:c + (k + 1) * P],
                                  yT_sb[:, k, 4 * h:4 * h + 4, :], k == 0, k == KD - 1)
                last.then_inc(t_sh, 1)

            shared(0)
            pe.wait_ge(v_chosen, 1)
            pe.wait_ge(v_qT1, NT)
            pe.wait_ge(p_const, 10)
            mm(T[1][:, 0:NT * E], before_b[:, :], chosen[:, :, :], True, False)
            for s in range(1, NT):
                last = mm(T[1][:, s * E:NT * E], ones_b[:, :], chosen[:, 0:NT - s, :], False, s == NT - 1)
            last.then_inc(t_rank, 1)
            for g in range(NT):
                last = mm(T[1][:, P:P + E], ones_b[:, :], chosen[:, g, :], g == 0, g == NT - 1)
            last.then_inc(t_tot, 1)
            shared(1)
            pe.wait_ge(v_comb, 1)
            for h in range(2):
                pe.wait_ge(v_yT, NT) if h == 0 else pe.wait_ge(v_combT, 1)
                for g in range(4):
                    last = nc.tensor.transpose(T[0][0:E + SH, g * P:(g + 1) * P], comb[:, 4 * h + g, :], ident_f[:, :])
                last.then_inc(t_combT, 1)
            shared(2)
            shared(3)
            for g in range(NT):
                pe.wait_ge(v_combT, 2)
                pe.wait_ge(v_shy, 4)
                if g >= 2:
                    pe.wait_ge(v_base, g - 1)
                else:
                    pe.wait_ge(a_y, NT)
                    pe.wait_ge(v_x1, NT)
                mm(S[g % 2][:, 0:D], combT[:, g, :], bdown_sb[:, :], True, False)
                for e in range(SH):
                    last = mm(S[g % 2][:, 0:D], shy[:, e, g * P:(g + 1) * P], wsh[:, e, DO:DO + D], False, e == SH - 1)
                last.then_inc(t_base, 1)

            def turn(t, s, n):
                pe.wait_ge(d_xr[s], 16 * (n + 1))
                if not (isinstance(t, int) and t < 2):
                    pe.wait_ge(v_xrT, t - 1)
                for k in range(KD):
                    last = nc.tensor.transpose(T_f(s % 2)[:, k, :], xr[:, s, k * P:(k + 1) * P], ident_f[:, :])
                last.then_inc(t_xr, 1)

            def up(t, s, n):
                pe.wait_ge(d_wr[s], 16 * (n + 1))
                pe.wait_ge(v_xrT, t + 1)
                if not (isinstance(t, int) and t < 2):
                    pe.wait_ge(v_yr, t - 1)
                for o, c in ((0, GO), (P, UO)):
                    for k in range(KD):
                        last = mm(M[s % 2][:, o:o + P], wr[:, s, c + k * P:c + (k + 1) * P], xrT[:, s % 2, k, :], k == 0, k == KD - 1)
                last.then_inc(t_gu, 1)

            def down(t, s, n):
                pe.wait_ge(v_yr, t + 1)
                if not (isinstance(t, int) and t < 2):
                    pe.wait_ge(a_rr, t - 1)
                mm(S[s % 2][:, 0:D], yr[:, s % 2, :], wr[:, s, DO:DO + D]).then_inc(t_dn, 1)

            pe.wait_ge(v_combT, 2)
            pe.wait_ge(v_base, NT)
            turn(0, 0, 0)
            for t in range(NS):
                if t + 1 < NS:
                    turn(t + 1, (t + 1) % RING, (t + 1) // RING)
                up(t, t % RING, t // RING)
                if t:
                    down(t - 1, (t - 1) % RING, (t - 1) // RING)
            down(NS - 1, (NS - 1) % RING, (NS - 1) // RING)


def pack_experts(g, u, d, gb, ub):
    n = g.shape[0]
    chunks = [w.reshape(n, KD, P, F).transpose(0, 2, 1, 3).reshape(n, P, KD * F) for w in (g, u)]
    return np.ascontiguousarray(np.concatenate(chunks + [d, gb[:, :, None], ub[:, :, None]], axis=2))


def kernel(**inputs):
    import concourse.bacc as bacc
    from concourse.bass_utils import run_bass_kernel_spmd

    v = {k: np.asarray(a) for k, a in inputs.items()}
    arrays = {
        "x": v["x"].reshape(B * C, D),
        "idx0": v["itok_B_0_7"],
        "idx1": v["itok_B_1_198"],
        "table0": np.concatenate([v["L0_cond_weights"].reshape(N0 * C, C), v["fside_8xS_0"].reshape(N0 * C, 1)], axis=1),
        "table1": v["L1_cond_weights"].reshape(N1 * C, C),
        "w1t": v["L0_ffn_w1"].T,
        "b1": v["L0_ffn_b1"],
        "w2t": v["L0_ffn_w2"].T,
        "b2": v["L0_ffn_b2"],
        "wa": v["L1_ffn_wa"],
        "wshared": pack_experts(*(v["L1_ffn_" + n] for n in ("sg", "sw1", "sw2", "sgb", "sb1"))),
        "wrouted": pack_experts(*(v["L1_ffn_" + n] for n in ("rg", "rw1", "rw2", "rgb", "rb1"))),
        "bdown": np.concatenate([v["L1_ffn_rb2"], v["L1_ffn_sb2"]], axis=0),
    }
    arrays = {k: np.ascontiguousarray(a) for k, a in arrays.items()}
    nc = bacc.Bacc("TRN2", target_bir_lowering=False, num_devices=1)
    args = [nc.dram_tensor(k, a.shape, mybir.dt.from_np(a.dtype), kind="ExternalInput").ap() for k, a in arrays.items()]
    out = nc.dram_tensor("out", [B * C, D], mybir.dt.float32, kind="ExternalOutput").ap()
    adaln_moe(nc, *args, out)
    r = run_bass_kernel_spmd(nc, [arrays], core_ids=[0])
    return r.results[0]["out"].reshape(B, C, D)
```

```python
import numpy as np
import concourse.bass as bass
from concourse import mybir
from contextlib import ExitStack

P = 128
B, C, D = 32, 32, 256
NT = B * C // P
BT = P // C
KD = D // P
F1 = 1024
KF = F1 // P
E, SH, TOPK = 16, 2, 2
F = 128
N0, N1 = 8, 200
EPS_RMS, EPS_Q, QMAX = 1e-6, 1e-5, 127.0
MAGIC = 1.5 * 2.0 ** 23
NS = (B * C * TOPK + E * (P - 1)) // P
RING = 4
WCOLS = 3 * D
DO = 2 * D


def gate_at(k):
    return 2 * F * k


def up_at(k):
    return 2 * F * k + F



def adaln_moe(nc, x, idx, table0, table1, w1t, b1, w2t, b2, wa, wshared, bshared, wrouted, brouted, bdown, out):
    f32, bf16, i32, u32 = mybir.dt.float32, mybir.dt.bfloat16, mybir.dt.int32, mybir.dt.uint32
    ALU, ACT, AX = mybir.AluOpType, mybir.ActivationFunctionType, mybir.AxisListType

    ctx = ExitStack()
    with ctx:
        def sb(name, shape, dt=f32):
            return ctx.enter_context(nc.sbuf_tensor(name, shape, dt))

        def ps(name, shape, dt=f32):
            return ctx.enter_context(nc.psum_tensor(name, shape, dt))

        def sem(name):
            return ctx.enter_context(nc.semaphore(name))

        def sems(name, n):
            return [sem(f"{name}{i}") for i in range(n)]

        slot_in = nc.dram_tensor("slot_in", [NS * P, D], f32).ap()
        slot_out = nc.dram_tensor("slot_out", [NS * P, D], f32).ap()

        idx_sb = sb("idx_sb", [P, 2, B], i32)
        pidx = sb("pidx", [P, 1], i32)
        cidx = sb("cidx", [P, 1], i32)
        rowidx = sb("rowidx", [P, 2, NT], i32)
        cond0 = sb("cond0", [P, NT, C + 1])
        cond1 = sb("cond1", [P, NT, C])
        blk0 = sb("blk0", [P, NT, P])
        blk1 = sb("blk1", [P, NT, P])
        blkmask = sb("blkmask", [P, BT])
        x_sb = sb("x_sb", [P, NT, D])
        xb_sb = sb("xb_sb", [P, NT, D])
        x1_sb = sb("x1_sb", [P, NT, D])
        y_sb = sb("y_sb", [P, NT, D])
        yT_sb = sb("yT_sb", [P, KD, NT, P])
        raw = sb("raw", [P, 2 * KD * F1])
        w1_sb = raw[:, 0:KD * F1].rearrange("p (k o) -> p k o", k=KD)
        w2_sb = raw[:, KD * F1:].rearrange("p (k o) -> p k o", k=KF)
        brow = raw[:, :].rearrange("p (e n) -> p e n", e=E)
        w1s = sb("w1s", [P, KD, F1], bf16)
        w2s = sb("w2s", [P, KF, D], bf16)
        wabs = sb("wabs", [P, 2])
        wmean = sb("wmean", [P, 2])
        b1_sb = sb("b1_sb", [P, F1])
        b2_sb = sb("b2_sb", [P, D])
        wa_sb = sb("wa_sb", [P, KD, E])
        bdown_sb = sb("bdown_sb", [E + SH, D])
        ones_f = sb("ones_f", [P, P])
        ones_b = sb("ones_b", [P, P], bf16)
        before_b = sb("before_b", [P, P], bf16)
        ident_f = sb("ident_f", [P, P])
        ident_b = sb("ident_b", [P, P], bf16)
        zeros = sb("zeros", [P, 1, D])
        h0 = sb("h0", [P, NT, D])
        junk = sb("junk", [P, F1])
        junk0 = sb("junk0", [P, 2, D])
        st = [sb(f"stats{n}", [P, 8, NT]) for n in range(2)]
        halfneg = sb("halfneg", [P, NT])
        arena = sb("arena", [P, (NT + 4) * F1])
        hid = arena[:, 0:NT * F1].rearrange("p (g n) -> p g n", n=F1)
        pre = arena[:, NT * F1:(NT + 2) * F1].rearrange("p (g n) -> p g n", n=F1)
        rq = arena[:, (NT + 2) * F1:].rearrange("p (g n) -> p g n", n=F1)
        wres = arena[:, :].rearrange("p (e n) -> p e n", n=WCOLS)
        picked = arena[:, 0:NT * TOPK * D].rearrange("p (g n) -> p g n", g=NT)
        rq0 = sb("rq0", [P, 2, D])
        qT0 = sb("qT0", [P, 2, KD, P], bf16)
        qT1 = sb("qT1", [P, 2, KF, P], bf16)
        aff = sb("aff", [P, NT, E])
        top = sb("top", [P, NT, 8])
        topi = sb("topi", [P, NT, 8], u32)
        topf = sb("topf", [P, NT, TOPK])
        prob = sb("prob", [P, NT, TOPK])
        psum2 = sb("psum2", [P, NT])
        oneh = sb("oneh", [P, NT, TOPK, E])
        onep = sb("onep", [P, NT, TOPK, E])
        chosen = sb("chosen", [P, NT, E], bf16)
        comb = sb("comb", [P, NT, E + SH])
        combT = sb("combT", [E + SH, NT, P])
        eidx = sb("eidx", [P, E])
        full = sb("full", [P, NT])
        tidx = sb("tidx", [P, NS])
        lower = sb("lower", [P, E, E])
        more = sb("more", [P, E, NT])
        ntile = sb("ntile", [P, E])
        prior = sb("prior", [P, E, E])
        first = sb("first", [P, E])
        endt = sb("endt", [P, E])
        firsts = sb("firsts", [P, E])
        place = sb("place", [P, NT, E])
        placed = sb("placed", [P, NT, TOPK, E])
        slotf = sb("slotf", [P, NT, TOPK])
        slot = sb("slot", [P, NT, TOPK], i32)
        past = sb("past", [P, NS, E])
        texf = sb("texf", [P, NS])
        tex = sb("tex", [P, NS], i32)
        wsh = sb("wsh", [P, SH, WCOLS])
        bsh = sb("bsh", [P, 2, SH])
        shg = sb("shg", [P, 2, 4 * P])
        shy = sb("shy", [P, SH, NT * P])
        base = x1_sb
        xr = x_sb[:, 0:RING, :]
        xrT = sb("xrT", [P, 2, KD, P])
        gub = sb("gub", [P, 2, 2 * F])
        gl = sb("gl", [P, 2, F])
        yr = sb("yr", [P, 2, F])
        yrT = sb("yrT", [P, 2, P])
        bt = sb("bt", [P, RING, 2 * F])
        rr = x_sb[:, RING:2 * RING, :]
        res = h0

        SS, AMAX, VAR, RINV, LIM, INV, SCALE, DEQ = range(8)

        S = [ps(f"S{i}", [P, 512]) for i in range(2)]
        T = [ps(f"T{i}", [P, 512]) for i in range(2)]
        M = [ps(f"M{i}", [P, 1024]) for i in range(2)]

        def T_f(i, n):
            return T[i][:, 0:n * P].rearrange("p (k m) -> p k m", m=P)

        def group(names):
            return (sem(n) for n in names.split())

        d_idx, d_x, d_w1, d_w2, d_b, d_bx, d_wa, d_wsh, d_zero, d_brow = group("d_idx d_x d_w1 d_w2 d_b d_bx d_wa d_wsh d_zero d_brow")
        d_cond0 = sems("d_cond0_", NT)
        d_cond1, d_scatter, d_out = group("d_cond1 d_scatter d_out")
        d_we, d_xr, d_rr = sems("d_we", E), sems("d_xr", RING), sems("d_rr", RING)
        d_pick = sems("d_pick", NT)
        p_const, p_pow, p_blk1, p_xb, p_own, p_bias = group("p_const p_pow p_blk1 p_xb p_own p_bias")
        v_own, v_zero, v_row, v_blk0, v_abs, v_mean, v_h0, v_max0, v_var, v_scale = group(
            "v_own v_zero v_row v_blk0 v_abs v_mean v_h0 v_max0 v_var v_scale")
        v_turned, v_pre, v_max1, v_x1, v_chosen, v_comb, v_slot, v_tex = group(
            "v_turned v_pre v_max1 v_x1 v_chosen v_comb v_slot v_tex")
        v_shy, v_base, v_xrT, v_gub, v_yr, v_res = group("v_shy v_base v_xrT v_gub v_yr v_res")
        a_sign, a_sq0, a_rq0, a_gelu, a_sq1, a_rq1, a_y, a_aff, a_shg, a_gl, a_yrT, a_rr = group(
            "a_sign a_sq0 a_rq0 a_gelu a_sq1 a_rq1 a_y a_aff a_shg a_gl a_yrT a_rr")
        t_mean, t_c0, t_turn, t_mm1, t_mm2, t_c1, t_logit, t_rank, t_tot = group(
            "t_mean t_c0 t_turn t_mm1 t_mm2 t_c1 t_logit t_rank t_tot")
        t_sh, t_base, t_xr, t_gu, t_yr, t_dn = group("t_sh t_base t_xr t_gu t_yr t_dn")

        HALF = NT // 2
        LAG_UP, LAG_GELU, LAG_Q1, LAG_DOWN, LAG_X1, LAG_C1, LAG_YT, LAG_LOGIT = 1, 2, 6, 7, 8, 9, 10, 11
        STEPS = NT + LAG_LOGIT

        def at(i, lag):
            return i - lag if 0 <= i - lag < NT else None

        turns = {}
        for i in range(STEPS):
            for kind, lag in (("q1a", LAG_DOWN), ("q1b", LAG_DOWN), ("y", LAG_YT), ("q0", 0)):
                if at(i, lag) is not None:
                    turns[kind, at(i, lag)] = len(turns)
        for h in range(2):
            turns["comb", h] = len(turns)

        block = ctx.enter_context(nc.Block())

        @block.sync
        def _(sp):
            sp.dma_start(idx_sb[:, :, :], idx.partition_broadcast(P)).then_inc(d_idx, 16)
            sp.dma_start(w1_sb, w1t.rearrange("(k p) o -> p k o", p=P)).then_inc(d_w1, 16)
            sp.dma_start(w2_sb, w2t.rearrange("(k p) o -> p k o", p=P)).then_inc(d_w2, 16)
            sp.dma_start(b1_sb[:, :], b1.partition_broadcast(P)).then_inc(d_b, 16)
            sp.dma_start(wa_sb[:, :, :], wa.rearrange("(k p) e -> p k e", p=P)).then_inc(d_wa, 16)
            sp.dma_start(bdown_sb[:, :], bdown).then_inc(d_wa, 16)
            for e in range(SH):
                sp.dma_start(wsh[:, e, :], wshared[e]).then_inc(d_wsh, 16)
            sp.dma_start(bsh[:, :, :], bshared).then_inc(d_wsh, 16)
            sp.wait_ge(v_zero, 1)
            sp.wait_ge(t_c0, HALF)
            sp.dma_start(slot_in.rearrange("(t p) d -> p t d", p=P),
                         zeros[:, :, :].to_broadcast([P, NS, D])).then_inc(d_zero, 16)
            sp.wait_ge(a_sign, 2)
            sp.wait_ge(v_abs, 2)
            sp.dma_start(brow, brouted.partition_broadcast(P)).then_inc(d_brow, 16)
            for e in range(E):
                last = ((e + 1) * WCOLS - 1) // F1
                sp.wait_ge(a_rq1, min(last + 1, NT))
                if last >= NT:
                    sp.wait_ge(a_gelu, NT)
                if last >= NT + 2:
                    sp.wait_ge(t_turn, turns["q1b", NT - 1] + 1)
                sp.dma_start(wres[:, e, :], wrouted[e]).then_inc(d_we[e], 16)

            def load(t, s, n):
                if n:
                    sp.wait_ge(t_xr, t - RING + 1)
                sp.dma_start(xr[:, s, :], slot_in[bass.ds(t * P, P), :]).then_inc(d_xr[s], 16)

            def store(t, s):
                sp.wait_ge(a_rr, t + 1)
                sp.dma_start(slot_out[bass.ds(t * P, P), :], rr[:, s, :]).then_inc(d_rr[s], 16)

            sp.wait_ge(d_scatter, 16 * NT * TOPK)
            for t in range(RING):
                load(t, t, 0)
            for i in range(NS + 3):
                if i + RING < NS:
                    load(i + RING, i % RING, i // RING + 1)
                if 0 <= (t := i - 3) < NS:
                    store(t, t % RING)
            for g in range(NT):
                sp.wait_ge(v_res, g + 1)
                sp.dma_start(out[g * P:(g + 1) * P, :], res[:, g, :]).then_inc(d_out, 16)
            sp.wait_ge(d_out, 16 * NT)

        @block.gpsimd
        def _(pool):
            nc.gpsimd.iota(pidx[:, :], [[0, 1]], base=0, channel_multiplier=1).then_inc(p_const, 1)
            own = 0

            def made(ins):
                nonlocal own
                own += 1
                ins.then_inc(p_own, 1)
                pool.wait_ge(p_own, own)

            made(nc.gpsimd.memset(blkmask[:, :], 1.0))
            made(nc.gpsimd.affine_select(out=blkmask[:, :], in_=blkmask[:, :], pattern=[[-C, BT]], compare_op=ALU.is_ge,
                                         fill=0.0, base=0, channel_multiplier=1))
            nc.gpsimd.affine_select(out=blkmask[:, :], in_=blkmask[:, :], pattern=[[C, BT]], compare_op=ALU.is_ge,
                                    fill=0.0, base=C - 1, channel_multiplier=-1).then_inc(p_const, 1)
            pool.wait_ge(v_row, 1)
            for g in range(NT):
                nc.gpsimd.indirect_dma_start(cond0[:, g, :], None, table0,
                                             bass.IndirectOffsetOnAxis(ap=rowidx[:, 0, g:g + 1], axis=0)).then_inc(d_cond0[g], 16)
            made(nc.gpsimd.memset(ident_f[:, :], 0.0))
            nc.gpsimd.affine_select(out=ident_f[:, :], in_=ident_f[:, :], pattern=[[-1, P]], compare_op=ALU.not_equal,
                                    fill=1.0, base=0, channel_multiplier=1).then_inc(p_const, 1)
            nc.gpsimd.memset(halfneg[:, :], -0.5).then_inc(p_const, 1)

            def inverse_root(layer, half):
                c = slice(half * HALF, (half + 1) * HALF)
                pool.wait_ge(v_var, 2 * layer + half + 1)
                nc.gpsimd.tensor_tensor(st[layer][:, RINV, c], st[layer][:, VAR, c], halfneg[:, c], ALU.pow).then_inc(p_pow, 1)

            for g in range(NT):
                nc.gpsimd.indirect_dma_start(cond1[:, g, :], None, table1,
                                             bass.IndirectOffsetOnAxis(ap=rowidx[:, 1, g:g + 1], axis=0)).then_inc(d_cond1, 16)
            pool.wait_ge(p_const, 4)
            inverse_root(0, 0)
            inverse_root(0, 1)
            made(nc.gpsimd.memset(before_b[:, :], 0.0))
            nc.gpsimd.affine_select(out=before_b[:, :], in_=before_b[:, :], pattern=[[-1, P]], compare_op=ALU.is_ge,
                                    fill=1.0, base=0, channel_multiplier=1).then_inc(p_const, 1)
            made(nc.gpsimd.memset(lower[:, :, :], 0.0))
            nc.gpsimd.affine_select(out=lower[:, :, :], in_=lower[:, :, :], pattern=[[-1, E], [1, E]], compare_op=ALU.is_ge,
                                    fill=1.0, base=0, channel_multiplier=0).then_inc(p_const, 1)
            nc.gpsimd.iota(eidx[:, :], [[1, E]], base=0, channel_multiplier=0,
                           allow_small_or_imprecise_dtypes=True).then_inc(p_const, 1)
            nc.gpsimd.iota(tidx[:, :], [[1, NS]], base=0, channel_multiplier=0,
                           allow_small_or_imprecise_dtypes=True).then_inc(p_const, 1)
            nc.gpsimd.iota(full[:, :], [[P, NT]], base=0, channel_multiplier=0,
                           allow_small_or_imprecise_dtypes=True).then_inc(p_const, 1)
            nc.gpsimd.memset(comb[:, :, E:E + SH], 1.0).then_inc(p_const, 1)
            pool.wait_ge(d_cond1, 16 * NT)
            for g in range(NT):
                nc.gpsimd.tensor_tensor(blk1[:, g, :].rearrange("p (q c) -> p q c", q=BT),
                                        cond1[:, g, :].unsqueeze(1).to_broadcast([P, BT, C]),
                                        blkmask[:, :].unsqueeze(2).to_broadcast([P, BT, C]), ALU.mult).then_inc(p_blk1, 1)
            pool.wait_ge(d_x, 32)
            pool.wait_ge(d_bx, 16)
            for g in range(NT):
                nc.gpsimd.tensor_tensor(xb_sb[:, g, :], x_sb[:, g, :], b2_sb[:, :], ALU.add).then_inc(p_xb, 1)
                if g == HALF - 1:
                    inverse_root(1, 0)
            inverse_root(1, 1)

            pool.wait_ge(v_slot, 1)
            pool.wait_ge(a_y, NT)
            pool.wait_ge(d_zero, 16)
            for g in range(NT):
                for k in range(TOPK):
                    nc.gpsimd.indirect_dma_start(slot_in, bass.IndirectOffsetOnAxis(ap=slot[:, g, k:k + 1], axis=0),
                                                 y_sb[:, g, :], None).then_inc(d_scatter, 16)
            pool.wait_ge(v_tex, 1)
            pool.wait_ge(d_brow, 16)
            for t in range(NS):
                if t % 8 == 0:
                    exs = nc.values_load_multi_w_load_instructions(
                        tex[0:1, t:min(t + 8, NS)], engines=[mybir.EngineType.Pool], min_val=0, max_val=E - 1,
                        skip_runtime_bounds_check_because="the routing keeps it below the number of experts")[1]
                e = exs[t % 8]
                if t >= RING:
                    pool.wait_ge(v_gub, t - RING + 1)
                nc.gpsimd.tensor_copy(bt[:, t % RING, :], brow[:, bass.ds(e, 1), :].rearrange("p a n -> p (a n)")).then_inc(p_bias, 1)
            for s in range(RING):
                pool.wait_ge(d_rr[s], 16 * len(range(s, NS, RING)))
            for g in range(NT):
                for k in range(TOPK):
                    nc.gpsimd.indirect_dma_start(picked[:, g, k * D:(k + 1) * D], None, slot_out,
                                                 bass.IndirectOffsetOnAxis(ap=slot[:, g, k:k + 1], axis=0)).then_inc(d_pick[g], 16)

        @block.scalar
        def _(act):
            act.dma_start(x_sb[:, 0:HALF, :], x[0:HALF * P].rearrange("(g p) d -> p g d", p=P)).then_inc(d_x, 16)
            act.dma_start(x_sb[:, HALF:NT, :], x[HALF * P:].rearrange("(g p) d -> p g d", p=P)).then_inc(d_x, 16)
            act.dma_start(b2_sb[:, :], b2.partition_broadcast(P)).then_inc(d_bx, 16)
            act.wait_ge(d_w1, 16)
            nc.scalar.activation(w1s[:, :, :], w1_sb, ACT.Sign).then_inc(a_sign, 1)

            def square0(g):
                act.wait_ge(v_h0, g + 1)
                if g >= 2:
                    act.wait_ge(a_sq0, g - 1)
                nc.scalar.activation(junk0[:, g % 2, :], h0[:, g, :], ACT.Square, accum_out=st[0][:, SS, g:g + 1]).then_inc(a_sq0, 1)

            for g in range(HALF):
                square0(g)
            for i in range(STEPS):
                if (g := at(i, LAG_GELU)) is not None:
                    act.wait_ge(v_pre, g + 1)
                    nc.scalar.activation(hid[:, g, :], pre[:, g % 2, :], ACT.Gelu).then_inc(a_gelu, 1)
                    act.wait_ge(a_gelu, g + 1)
                    nc.scalar.activation(junk[:, :], hid[:, g, :], ACT.Square, accum_out=st[1][:, SS, g:g + 1]).then_inc(a_sq1, 1)
                if (g := at(i, 0)) is not None:
                    act.wait_ge(v_scale, g // HALF + 1)
                    if g >= 2:
                        act.wait_ge(t_turn, turns["q0", g - 2] + 1)
                    nc.scalar.activation(rq0[:, g % 2, :], h0[:, g, :], ACT.Copy, bias=MAGIC,
                                         scale=st[0][:, SCALE, g:g + 1]).then_inc(a_rq0, 1)
                    if g < HALF:
                        square0(g + HALF)
                    if g == 0:
                        act.wait_ge(d_w2, 16)
                        nc.scalar.activation(w2s[:, :, :], w2_sb, ACT.Sign).then_inc(a_sign, 1)
                if (g := at(i, LAG_C1)) is not None:
                    act.wait_ge(t_c1, g + 1)
                    nc.scalar.activation(y_sb[:, g, :], S[1][:, 0:D], ACT.Copy).then_inc(a_y, 1)
                if (g := at(i, LAG_Q1)) is not None:
                    act.wait_ge(v_scale, g // HALF + 3)
                    if g >= 2:
                        act.wait_ge(t_turn, turns["q1b", g - 2] + 1)
                    nc.scalar.activation(rq[:, g % 2, :], hid[:, g, :], ACT.Copy, bias=MAGIC,
                                         scale=st[1][:, SCALE, g:g + 1]).then_inc(a_rq1, 1)
            act.wait_ge(t_logit, NT)
            nc.scalar.activation(aff[:, :, :], M[0][:, 0:NT * E].rearrange("p (g e) -> p g e", e=E), ACT.Sigmoid).then_inc(a_aff, 1)
            act.wait_ge(d_wsh, 16 * (SH + 1))
            for n in range(2 * SH):
                act.wait_ge(t_sh, n + 1)
                if n >= 2:
                    act.wait_ge(v_shy, n - 1)
                nc.scalar.activation(shg[:, n % 2, :], M[1 - n % 2][:, 0:4 * P], ACT.Gelu,
                                     bias=bsh[:, 0, n % SH:n % SH + 1]).then_inc(a_shg, 1)

            def gate(t, b, first):
                act.wait_ge(v_gub, t + 1)
                if not first:
                    act.wait_ge(v_yr, t - 1)
                nc.scalar.activation(gl[:, b, :], gub[:, b, 0:F], ACT.Gelu).then_inc(a_gl, 1)

            def turned(t, b, first):
                act.wait_ge(t_yr, t + 1)
                if not first:
                    act.wait_ge(t_dn, t - 1)
                nc.scalar.activation(yrT[:, b, :], M[1][:, b * 512:b * 512 + P], ACT.Copy).then_inc(a_yrT, 1)

            def rows(t, b, s, n):
                act.wait_ge(t_dn, t + 1)
                if n:
                    act.wait_ge(d_rr[s], 16 * n)
                nc.scalar.activation(rr[:, s, :], S[b][:, 0:D], ACT.Copy).then_inc(a_rr, 1)

            for i in range(NS + 3):
                if 0 <= (t := i - 3) < NS:
                    rows(t, t % 2, t % RING, t // RING)
                if 0 <= (t := i - 2) < NS:
                    turned(t, t % 2, t < 2)
                if 0 <= (t := i) < NS:
                    gate(t, t % 2, t < 2)

        @block.vector
        def _(dve):
            own = 0

            def then(ins):
                nonlocal own
                own += 1
                ins.then_inc(v_own, 1)
                dve.wait_ge(v_own, own)

            dve.wait_ge(p_const, 1)
            then(nc.vector.tensor_scalar(cidx[:, :], pidx[:, :], C - 1, None, ALU.bitwise_and))
            nc.vector.memset(zeros[:, :, :], 0.0).then_inc(v_zero, 1)
            nc.vector.memset(ones_b[:, :], 1.0)
            nc.vector.memset(ones_f[:, :], 1.0).then_inc(v_zero, 1)
            dve.wait_ge(d_idx, 16)
            for b in range(BT):
                r = slice(b * C, (b + 1) * C)
                last = nc.vector.tensor_scalar(rowidx[r, :, :], idx_sb[r, :, :].rearrange("p l (g b) -> p l g b", b=BT)[:, :, :, b],
                                               float(C), cidx[r, :], ALU.mult, ALU.add)
            last.then_inc(v_row, 1)
            dve.wait_ge(p_const, 2)

            def block0(g):
                dve.wait_ge(d_cond0[g], 16)
                nc.vector.tensor_tensor(blk0[:, g, :].rearrange("p (q c) -> p q c", q=BT),
                                        cond0[:, g, 0:C].unsqueeze(1).to_broadcast([P, BT, C]),
                                        blkmask[:, :].unsqueeze(2).to_broadcast([P, BT, C]), ALU.mult).then_inc(v_blk0, 1)

            def stats0(g):
                dve.wait_ge(t_c0, g + 1)
                nc.vector.tensor_scalar(h0[:, g, :], S[g % 2][:, 0:D], cond0[:, g, C:C + 1], None, ALU.add).then_inc(v_h0, 1)
                dve.wait_ge(v_h0, g + 1)
                nc.vector.tensor_reduce(st[0][:, AMAX, g:g + 1], h0[:, g, :], AX.X, ALU.max, apply_absolute_value=True).then_inc(v_max0, 1)

            def abs_sum(n, w, d):
                dve.wait_ge(d, 16)
                nc.vector.tensor_reduce(wabs[:, n:n + 1], w, AX.XY, ALU.add, apply_absolute_value=True).then_inc(v_abs, 1)

            def mean(n):
                dve.wait_ge(t_mean, n + 1)
                nc.vector.tensor_scalar(wmean[:, n:n + 1], (M[0], S[1])[n][:, n:n + 1], 1.0 / (D * F1), None, ALU.mult).then_inc(v_mean, 1)
                dve.wait_ge(v_mean, n + 1)

            def scales(layer, half, width):
                c = slice(half * HALF, (half + 1) * HALF)
                s = st[layer]
                dve.wait_ge((a_sq0, a_sq1)[layer], (half + 1) * HALF)
                nc.vector.tensor_scalar(s[:, VAR, c], s[:, SS, c], 1.0 / width, EPS_RMS, ALU.mult, ALU.add).then_inc(v_var, 1)
                dve.wait_ge(p_pow, 2 * layer + half + 1)
                dve.wait_ge((v_max0, v_max1)[layer], (half + 1) * HALF)
                then(nc.vector.tensor_tensor(s[:, LIM, c], s[:, AMAX, c], s[:, RINV, c], ALU.mult))
                then(nc.vector.tensor_scalar(s[:, LIM, c], s[:, LIM, c], width ** -0.5, EPS_Q, ALU.mult, ALU.max))
                then(nc.vector.reciprocal(s[:, INV, c], s[:, LIM, c]))
                then(nc.vector.tensor_scalar(s[:, INV, c], s[:, INV, c], QMAX * width ** -0.5, None, ALU.mult))
                nc.vector.tensor_tensor(s[:, SCALE, c], s[:, INV, c], s[:, RINV, c], ALU.mult).then_inc(v_scale, 1)
                then(nc.vector.tensor_scalar(s[:, DEQ, c], s[:, LIM, c], wmean[:, layer:layer + 1], 1.0 / QMAX, ALU.mult, ALU.mult))

            def turned(kind, g, dst, n, rounded):
                u = turns[kind, g]
                dve.wait_ge(t_turn, u + 1)
                if rounded:
                    nc.vector.tensor_scalar(dst, T_f(u % 2, n), -MAGIC, None, ALU.add).then_inc(v_turned, 1)
                else:
                    nc.vector.tensor_copy(dst, T_f(u % 2, n)).then_inc(v_turned, 1)

            abs_sum(0, w1_sb, d_w1)
            block0(0)
            block0(1)
            for g in range(HALF):
                if g + 2 < NT:
                    block0(g + 2)
                stats0(g)
            mean(0)
            scales(0, 0, D)
            for g in range(HALF + 2, NT):
                block0(g)
            dve.wait_ge(d_b, 16)
            for i in range(STEPS):
                if (g := at(i, LAG_DOWN)) is not None:
                    if g >= 2:
                        dve.wait_ge(t_mm2, g - 1)
                    turned("q1a", g, qT1[:, g % 2, 0:4, :], 4, True)
                    turned("q1b", g, qT1[:, g % 2, 4:8, :], 4, True)
                if (g := at(i, LAG_UP)) is not None:
                    dve.wait_ge(t_mm1, g + 1)
                    if g >= 2:
                        dve.wait_ge(a_gelu, g - 1)
                    nc.vector.scalar_tensor_tensor(pre[:, g % 2, :], M[g % 2][:, :], st[0][:, DEQ, g:g + 1], b1_sb[:, :],
                                                   ALU.mult, ALU.add).then_inc(v_pre, 1)
                if (g := at(i, LAG_X1)) is not None:
                    dve.wait_ge(t_mm2, g + 1)
                    dve.wait_ge(p_xb, g + 1)
                    nc.vector.scalar_tensor_tensor(x1_sb[:, g, :], S[0][:, 0:D], st[1][:, DEQ, g:g + 1], xb_sb[:, g, :],
                                                   ALU.mult, ALU.add).then_inc(v_x1, 1)
                if (g := at(i, LAG_YT)) is not None:
                    turned("y", g, yT_sb[:, :, g, :], KD, False)
                if i < HALF:
                    stats0(HALF + i)
                    if i == 1:
                        abs_sum(1, w2_sb, d_w2)
                    if i == HALF - 1:
                        scales(0, 1, D)
                if (g := at(i, 0)) is not None:
                    if g >= 2:
                        dve.wait_ge(t_mm1, g - 1)
                    turned("q0", g, qT0[:, g % 2, :, :], KD, True)
                if (g := at(i, LAG_GELU)) is not None:
                    dve.wait_ge(a_gelu, g + 1)
                    nc.vector.tensor_reduce(st[1][:, AMAX, g:g + 1], hid[:, g, :], AX.X, ALU.max, apply_absolute_value=True).then_inc(v_max1, 1)
                    if g == HALF - 1:
                        mean(1)
                    if g % HALF == HALF - 1:
                        scales(1, g // HALF, F1)

            dve.wait_ge(a_aff, 1)
            for g in range(NT):
                last = nc.vector.max(top[:, g, :], aff[:, g, :])
            then(last)
            for g in range(NT):
                last = nc.vector.max_index(topi[:, g, :], top[:, g, :], aff[:, g, :])
            then(last)
            then(nc.vector.tensor_copy(topf[:, :, :], topi[:, :, 0:TOPK]))
            dve.wait_ge(p_const, 10)
            then(nc.vector.tensor_tensor(oneh[:, :, :, :], topf[:, :, :].unsqueeze(3).to_broadcast([P, NT, TOPK, E]),
                                         eidx[:, :].unsqueeze(1).unsqueeze(1).to_broadcast([P, NT, TOPK, E]), ALU.is_equal))
            nc.vector.tensor_tensor(chosen[:, :, :], oneh[:, :, 0, :], oneh[:, :, 1, :], ALU.add).then_inc(v_chosen, 1)
            then(nc.vector.tensor_tensor(psum2[:, :], top[:, :, 0], top[:, :, 1], ALU.add))
            then(nc.vector.reciprocal(psum2[:, :], psum2[:, :]))
            then(nc.vector.tensor_tensor(prob[:, :, :], top[:, :, 0:TOPK], psum2[:, :].unsqueeze(2).to_broadcast([P, NT, TOPK]), ALU.mult))
            then(nc.vector.tensor_tensor(onep[:, :, :, :], oneh[:, :, :, :], prob[:, :, :].unsqueeze(3).to_broadcast([P, NT, TOPK, E]), ALU.mult))
            nc.vector.tensor_tensor(comb[:, :, 0:E], onep[:, :, 0, :], onep[:, :, 1, :], ALU.add).then_inc(v_comb, 1)
            dve.wait_ge(t_tot, 1)
            then(nc.vector.tensor_tensor(more[:, :, :], S[1][:, P:P + E].unsqueeze(2).to_broadcast([P, E, NT]),
                                         full[:, :].unsqueeze(1).to_broadcast([P, E, NT]), ALU.is_gt))
            then(nc.vector.tensor_reduce(ntile[:, :], more[:, :, :], AX.X, ALU.add))
            then(nc.vector.tensor_tensor(prior[:, :, :], ntile[:, :].unsqueeze(1).to_broadcast([P, E, E]), lower[:, :, :], ALU.mult))
            then(nc.vector.tensor_reduce(first[:, :], prior[:, :, :], AX.X, ALU.add))
            then(nc.vector.tensor_scalar(firsts[:, :], first[:, :], float(P), None, ALU.mult))
            then(nc.vector.tensor_tensor(place[:, :, :], S[1][:, 0:NT * E].rearrange("p (g e) -> p g e", e=E),
                                         firsts[:, :].unsqueeze(1).to_broadcast([P, NT, E]), ALU.add))
            then(nc.vector.tensor_tensor(placed[:, :, :, :], oneh[:, :, :, :],
                                         place[:, :, :].unsqueeze(2).to_broadcast([P, NT, TOPK, E]), ALU.mult))
            then(nc.vector.tensor_reduce(slotf[:, :, :], placed[:, :, :, :], AX.X, ALU.add))
            nc.vector.tensor_copy(slot[:, :, :], slotf[:, :, :]).then_inc(v_slot, 1)
            then(nc.vector.tensor_tensor(endt[:, :], first[:, :], ntile[:, :], ALU.add))
            then(nc.vector.tensor_tensor(past[:, :, :], endt[:, :].unsqueeze(1).to_broadcast([P, NS, E]),
                                         tidx[:, :].unsqueeze(2).to_broadcast([P, NS, E]), ALU.is_le))
            then(nc.vector.tensor_reduce(texf[:, :], past[:, :, :], AX.X, ALU.add))
            nc.vector.tensor_scalar(tex[:, :], texf[:, :], E - 1.0, None, ALU.min).then_inc(v_tex, 1)

            for h in range(2):
                u = turns["comb", h]
                dve.wait_ge(t_turn, u + 1)
                nc.vector.tensor_copy(combT[:, h * 4:(h + 1) * 4, :], T_f(u % 2, 4)[0:E + SH]).then_inc(v_turned, 1)
            for n in range(2 * SH):
                dve.wait_ge(a_shg, n + 1)
                nc.vector.scalar_tensor_tensor(shy[:, n % SH, (n // SH) * 4 * P:(n // SH + 1) * 4 * P], M[1 - n % 2][:, 4 * P:8 * P],
                                               bsh[:, 1, n % SH:n % SH + 1], shg[:, n % 2, :], ALU.add, ALU.mult).then_inc(v_shy, 1)
            for g in range(NT):
                then(nc.vector.tensor_tensor(base[:, g, :], x1_sb[:, g, :], y_sb[:, g, :], ALU.add))
                dve.wait_ge(t_base, g + 1)
                nc.vector.tensor_tensor(base[:, g, :], base[:, g, :], S[g % 2][:, 0:D], ALU.add).then_inc(v_base, 1)

            def rows_turned(t, b, first):
                dve.wait_ge(t_xr, t + 1)
                if not first:
                    dve.wait_ge(t_gu, t - 1)
                nc.vector.tensor_copy(xrT[:, b, :, :], T_f(b, KD)).then_inc(v_xrT, 1)

            def biased(t, b, s, first):
                dve.wait_ge(t_gu, t + 1)
                dve.wait_ge(p_bias, t + 1)
                if not first:
                    dve.wait_ge(a_gl, t - 1)
                nc.vector.tensor_tensor(gub[:, b, :], M[0][:, b * 512:b * 512 + 2 * F], bt[:, s, :], ALU.add).then_inc(v_gub, 1)

            def gated(t, b, first):
                dve.wait_ge(a_gl, t + 1)
                if not first:
                    dve.wait_ge(t_yr, t - 1)
                nc.vector.tensor_tensor(yr[:, b, :], gub[:, b, F:2 * F], gl[:, b, :], ALU.mult).then_inc(v_yr, 1)

            for i in range(-1, NS + 1):
                if 0 <= (t := i + 1) < NS:
                    rows_turned(t, t % 2, t < 2)
                if 0 <= (t := i - 1) < NS:
                    gated(t, t % 2, t < 2)
                if 0 <= (t := i) < NS:
                    biased(t, t % 2, t % RING, t < 2)
            for g in range(NT):
                dve.wait_ge(d_pick[g], 32)
                then(nc.vector.scalar_tensor_tensor(base[:, g, :], picked[:, g, 0:D], prob[:, g, 0:1], base[:, g, :], ALU.mult, ALU.add))
                nc.vector.scalar_tensor_tensor(res[:, g, :], picked[:, g, D:2 * D], prob[:, g, 1:2], base[:, g, :],
                                               ALU.mult, ALU.add).then_inc(v_res, 1)

        @block.tensor
        def _(pe):
            def mm(o, l, r, start=True, stop=True):
                return nc.tensor.matmul(o, l, r, start=start, stop=stop)

            def turn(kind, g, blocks, rows=P):
                u = turns[kind, g]
                if u >= 2:
                    pe.wait_ge(v_turned, u - 1)
                for k, b in enumerate(blocks):
                    last = nc.tensor.transpose(T_f(u % 2, len(blocks))[0:rows, k, :], b, ident_f[:, :])
                last.then_inc(t_turn, 1)

            def mean(n):
                pe.wait_ge(v_abs, n + 1)
                mm((M[0], S[1])[n][:, n:n + 1], ones_f[:, :], wabs[:, n:n + 1]).then_inc(t_mean, 1)

            def condition0(g):
                pe.wait_ge(v_blk0, g + 1)
                if g >= 2:
                    pe.wait_ge(v_h0, g - 1)
                mm(S[g % 2][:, 0:D], blk0[:, g, :], x_sb[:, g, :]).then_inc(t_c0, 1)

            pe.wait_ge(v_zero, 2)
            mean(0)
            pe.wait_ge(d_x, 32)
            for g in range(HALF):
                condition0(g)
            pe.wait_ge(p_const, 3)
            pe.wait_ge(a_sign, 1)
            for i in range(STEPS):
                if i < HALF:
                    condition0(HALF + i)
                if (g := at(i, LAG_DOWN)) is not None:
                    pe.wait_ge(a_rq1, g + 1)
                    for n, kind in enumerate(("q1a", "q1b")):
                        turn(kind, g, [rq[:, g % 2, k * P:(k + 1) * P] for k in range(4 * n, 4 * n + 4)])
                if (g := at(i, LAG_UP)) is not None:
                    pe.wait_ge(v_turned, turns["q0", g] + 1)
                    if g >= 2:
                        pe.wait_ge(v_pre, g - 1)
                    if g == 0:
                        pe.wait_ge(v_mean, 1)
                    for n in range(2):
                        for k in range(KD):
                            last = mm(M[g % 2][:, n * 512:(n + 1) * 512], qT0[:, g % 2, k, :], w1s[:, k, n * 512:(n + 1) * 512],
                                      k == 0, k == KD - 1)
                    last.then_inc(t_mm1, 1)
                if (g := at(i, LAG_C1)) is not None:
                    pe.wait_ge(v_x1, g + 1)
                    pe.wait_ge(p_blk1, g + 1)
                    if g:
                        pe.wait_ge(a_y, g)
                    else:
                        pe.wait_ge(v_mean, 2)
                    mm(S[1][:, 0:D], blk1[:, g, :], x1_sb[:, g, :]).then_inc(t_c1, 1)
                if (g := at(i, LAG_DOWN)) is not None:
                    pe.wait_ge(v_turned, turns["q1b", g] + 1)
                    pe.wait_ge(a_sign, 2)
                    if g:
                        pe.wait_ge(v_x1, g)
                    for k in range(KF):
                        last = mm(S[0][:, 0:D], qT1[:, g % 2, k, :], w2s[:, k, :], k == 0, k == KF - 1)
                    last.then_inc(t_mm2, 1)
                if (g := at(i, LAG_YT)) is not None:
                    pe.wait_ge(a_y, g + 1)
                    turn("y", g, [y_sb[:, g, k * P:(k + 1) * P] for k in range(KD)])
                if (g := at(i, 0)) is not None:
                    pe.wait_ge(a_rq0, g + 1)
                    turn("q0", g, [rq0[:, g % 2, k * P:(k + 1) * P] for k in range(KD)])
                    if g == HALF:
                        pe.wait_ge(v_h0, NT)
                        mean(1)
                if (g := at(i, LAG_LOGIT)) is not None:
                    pe.wait_ge(v_turned, turns["y", g] + 1)
                    pe.wait_ge(v_pre, NT)
                    pe.wait_ge(d_wa, 32)
                    for k in range(KD):
                        last = mm(M[0][:, g * E:(g + 1) * E], yT_sb[:, k, g, :], wa_sb[:, k, :], k == 0, k == KD - 1)
                    last.then_inc(t_logit, 1)

            pe.wait_ge(d_wsh, 16 * (SH + 1))

            def shared(n):
                e, h = n % SH, n // SH
                if n >= 2:
                    pe.wait_ge(v_shy, n - 1)
                elif n == 1:
                    pe.wait_ge(a_aff, 1)
                for o, at_ in ((0, gate_at), (4 * P, up_at)):
                    for k in range(KD):
                        last = mm(M[1 - n % 2][:, o:o + 4 * P], wsh[:, e, at_(k):at_(k) + F],
                                  yT_sb[:, k, 4 * h:4 * h + 4, :], k == 0, k == KD - 1)
                last.then_inc(t_sh, 1)

            shared(0)
            shared(1)
            pe.wait_ge(v_chosen, 1)
            pe.wait_ge(a_y, NT)
            pe.wait_ge(p_const, 10)
            mm(S[1][:, 0:NT * E], before_b[:, :], chosen[:, :, :], True, False)
            for s in range(1, NT):
                last = mm(S[1][:, s * E:NT * E], ones_b[:, :], chosen[:, 0:NT - s, :], False, s == NT - 1)
            last.then_inc(t_rank, 1)
            for g in range(NT):
                last = mm(S[1][:, P:P + E], ones_b[:, :], chosen[:, g, :], g == 0, g == NT - 1)
            last.then_inc(t_tot, 1)
            pe.wait_ge(v_comb, 1)
            for h in range(2):
                turn("comb", h, [comb[:, 4 * h + g, :] for g in range(4)], E + SH)
            shared(2)
            shared(3)
            pe.wait_ge(v_turned, turns["comb", 1] + 1)
            pe.wait_ge(v_shy, 4)
            for g in range(NT):
                if g >= 2:
                    pe.wait_ge(v_base, g - 1)
                else:
                    pe.wait_ge(v_slot, 1)
                mm(S[g % 2][:, 0:D], combT[:, g, :], bdown_sb[:, :], True, False)
                for e in range(SH):
                    last = mm(S[g % 2][:, 0:D], shy[:, e, g * P:(g + 1) * P], wsh[:, e, DO:DO + D], False, e == SH - 1)
                last.then_inc(t_base, 1)

            def turn_rows(t, b, s, n, first):
                pe.wait_ge(d_xr[s], 16 * (n + 1))
                if not first:
                    pe.wait_ge(v_xrT, t - 1)
                for k in range(KD):
                    last = nc.tensor.transpose(T_f(b, KD)[:, k, :], xr[:, s, k * P:(k + 1) * P], ident_f[:, :])
                last.then_inc(t_xr, 1)

            def experts(t, n):
                return nc.values_load_multi_w_load_instructions(
                    tex[0:1, t:t + n], engines=[mybir.EngineType.PE], min_val=0, max_val=E - 1,
                    skip_runtime_bounds_check_because="the routing keeps it below the number of experts")[1]

            def up(t, b, e, first):
                pe.wait_ge(v_xrT, t + 1)
                if not first:
                    pe.wait_ge(v_gub, t - 1)
                for k in range(KD):
                    last = mm(M[0][:, b * 512:b * 512 + 2 * F], xrT[:, b, k, :],
                              wres[:, bass.ds(e, 1), gate_at(k):gate_at(k) + 2 * F].rearrange("p a n -> p (a n)"), k == 0, k == KD - 1)
                last.then_inc(t_gu, 1)

            def turn_gated(t, b, first):
                pe.wait_ge(v_yr, t + 1)
                if not first:
                    pe.wait_ge(a_yrT, t - 1)
                nc.tensor.transpose(M[1][:, b * 512:b * 512 + P], yr[:, b, :], ident_f[:, :]).then_inc(t_yr, 1)

            def down(t, b, e, first):
                pe.wait_ge(a_yrT, t + 1)
                if not first:
                    pe.wait_ge(a_rr, t - 1)
                mm(S[b][:, 0:D], yrT[:, b, :], wres[:, bass.ds(e, 1), DO:DO + D].rearrange("p a n -> p (a n)")).then_inc(t_dn, 1)

            pe.wait_ge(v_base, NT)
            pe.wait_ge(v_tex, 1)
            for e in range(E):
                pe.wait_ge(d_we[e], 16)
            ex = {}
            turn_rows(0, 0, 0, 0, True)
            for i in range(NS + 3):
                if i < NS and i % 8 == 0:
                    n = min(8, NS - i)
                    ex.update(zip(range(i, i + n), experts(i, n)))
                if (t := i + 1) < NS:
                    turn_rows(t, t % 2, t % RING, t // RING, t < 2)
                if (t := i) < NS:
                    up(t, t % 2, ex[t], t < 2)
                if 0 <= (t := i - 2) < NS:
                    turn_gated(t, t % 2, t < 2)
                if 0 <= (t := i - 3) < NS:
                    down(t, t % 2, ex.pop(t), t < 2)


def pack_experts(g, u, d):
    n = g.shape[0]
    gu = np.stack([w.reshape(n, KD, P, F) for w in (g, u)], axis=3)
    return np.concatenate([gu.transpose(0, 2, 1, 3, 4).reshape(n, P, 2 * KD * F), d], axis=2)


def kernel(**inputs):
    import concourse.bacc as bacc
    from concourse.bass_utils import run_bass_kernel_spmd

    v = {k: np.asarray(a) for k, a in inputs.items()}
    arrays = {
        "x": v["x"].reshape(B * C, D),
        "idx": np.stack([v["itok_B_0_7"], v["itok_B_1_198"]]),
        "table0": np.concatenate([v["L0_cond_weights"].reshape(N0 * C, C), v["fside_8xS_0"].reshape(N0 * C, 1)], axis=1),
        "table1": v["L1_cond_weights"].reshape(N1 * C, C),
        "w1t": v["L0_ffn_w1"].T,
        "b1": v["L0_ffn_b1"],
        "w2t": v["L0_ffn_w2"].T,
        "b2": v["L0_ffn_b2"],
        "wa": v["L1_ffn_wa"],
        "wshared": pack_experts(*(v["L1_ffn_" + n] for n in ("sg", "sw1", "sw2"))),
        "bshared": np.stack([v["L1_ffn_sgb"].T, v["L1_ffn_sb1"].T], axis=1),
        "wrouted": pack_experts(*(v["L1_ffn_" + n] for n in ("rg", "rw1", "rw2"))),
        "brouted": np.stack([v["L1_ffn_rgb"], v["L1_ffn_rb1"]], axis=1).reshape(E, 2 * F),
        "bdown": np.concatenate([v["L1_ffn_rb2"], v["L1_ffn_sb2"]], axis=0),
    }
    arrays = {k: np.ascontiguousarray(a) for k, a in arrays.items()}
    nc = bacc.Bacc("TRN2", target_bir_lowering=False, num_devices=1)
    args = [nc.dram_tensor(k, a.shape, mybir.dt.from_np(a.dtype), kind="ExternalInput").ap() for k, a in arrays.items()]
    out = nc.dram_tensor("out", [B * C, D], mybir.dt.float32, kind="ExternalOutput").ap()
    adaln_moe(nc, *args, out)
    r = run_bass_kernel_spmd(nc, [arrays], core_ids=[0])
    return r.results[0]["out"].reshape(B, C, D)
```

```python
import numpy as np
import concourse.bass as bass
from concourse import mybir
from contextlib import ExitStack

P = 128
B, C, D = 32, 32, 256
NT = B * C // P
BT = P // C
KD = D // P
F1 = 1024
KF = F1 // P
E, SH, TOPK = 16, 2, 2
F = 128
N0, N1 = 8, 200
EPS_RMS, EPS_Q, QMAX = 1e-6, 1e-5, 127.0
MAGIC = 1.5 * 2.0 ** 23
REGION = P + B * C
NS = (B * C * TOPK + E * (P - 1)) // P
GROUP = 2
REST_FROM = NS + 1
LAG_SUM = 6
POOL_SUMS = (0, 3, 5)
RING = 4
WCOLS = 3 * D
DO = 2 * D
SECOND, PLACE, ROW = D, D + 1, D + 2


def gate_at(k):
    return 2 * F * k


def up_at(k):
    return 2 * F * k + F


def adaln_moe(nc, x, idx, table0, table1, w1t, b1, w2t, b2, wa, wshared, bshared, wrouted, brouted, bdown, out):
    f32, bf16, i32, u32 = mybir.dt.float32, mybir.dt.bfloat16, mybir.dt.int32, mybir.dt.uint32
    ALU, ACT, AX = mybir.AluOpType, mybir.ActivationFunctionType, mybir.AxisListType

    ctx = ExitStack()
    with ctx:
        def sb(name, shape, dt=f32):
            return ctx.enter_context(nc.sbuf_tensor(name, shape, dt))

        def ps(name, shape, dt=f32):
            return ctx.enter_context(nc.psum_tensor(name, shape, dt))

        def sem(name):
            return ctx.enter_context(nc.semaphore(name))

        def sems(name, n):
            return [sem(f"{name}{i}") for i in range(n)]

        slot_in = nc.dram_tensor("slot_in", [E * REGION, ROW], f32).ap()
        token_out = nc.dram_tensor("token_out", [NT * P * TOPK + NS * P, D], f32).ap()

        idx_sb = sb("idx_sb", [P, 2, B], i32)
        pidx = sb("pidx", [P, 1], i32)
        cidx = sb("cidx", [P, 1], i32)
        rowidx = sb("rowidx", [P, 2, NT], i32)
        cond0 = sb("cond0", [P, NT, C + 1])
        cond1 = sb("cond1", [P, NT, C])
        blk0 = sb("blk0", [P, NT, P])
        blk1 = sb("blk1", [P, NT, P])
        blkmask = sb("blkmask", [P, BT])
        x_sb = sb("x_sb", [P, NT, D])
        x1_sb = sb("x1_sb", [P, NT, D])
        y_sb = sb("y_sb", [P, NT, ROW])
        yT_sb = sb("yT_sb", [P, KD, NT, P])
        raw = sb("raw", [P, 2 * KD * F1])
        w1_sb = raw[:, 0:KD * F1].rearrange("p (k o) -> p k o", k=KD)
        w2_sb = raw[:, KD * F1:].rearrange("p (k o) -> p k o", k=KF)
        brow = raw[:, :].rearrange("p (e n) -> p e n", e=E)
        w1s = sb("w1s", [P, KD, F1], bf16)
        w2s = sb("w2s", [P, KF, D], bf16)
        wabs = sb("wabs", [P, 2])
        wmean = sb("wmean", [P, 2])
        b1_sb = sb("b1_sb", [P, F1])
        b2_sb = sb("b2_sb", [P, D])
        wa_sb = sb("wa_sb", [P, KD, E])
        bdown_sb = sb("bdown_sb", [P, E + SH, D])
        bshared_sum = sb("bshared_sum", [P, D])
        ones_f = sb("ones_f", [P, P])
        ones_b = sb("ones_b", [P, P], bf16)
        before_b = sb("before_b", [P, P], bf16)
        ident_f = sb("ident_f", [P, P])
        empty = sb("empty", [P, 1, ROW])
        spare = sb("spare", [P, NS])
        h0 = sb("h0", [P, NT, D])
        junk = sb("junk", [P, F1])
        junk0 = sb("junk0", [P, 2, D])
        st = [sb(f"stats{n}", [P, 8, NT]) for n in range(2)]
        halfneg = sb("halfneg", [P, NT])
        arena = sb("arena", [P, (NT + 4) * F1])
        hid = arena[:, 0:NT * F1].rearrange("p (g n) -> p g n", n=F1)
        pre = arena[:, NT * F1:(NT + 2) * F1].rearrange("p (g n) -> p g n", n=F1)
        rq = arena[:, (NT + 2) * F1:].rearrange("p (g n) -> p g n", n=F1)
        wres = arena[:, :].rearrange("p (e n) -> p e n", n=WCOLS)
        picked = arena[:, 0:NT * TOPK * D].rearrange("p (g n) -> p g n", g=NT)
        warm = sb("warm", [P, 2])
        rq0 = sb("rq0", [P, 2, D])
        qT0 = sb("qT0", [P, 2, KD, P], bf16)
        qT1 = sb("qT1", [P, 2, KF, P], bf16)
        aff = sb("aff", [P, NT, E])
        top = sb("top", [P, NT, 8])
        topi = sb("topi", [P, NT, 8], u32)
        topf = sb("topf", [P, NT, TOPK])
        prob = sb("prob", [P, NT, TOPK])
        psum2 = sb("psum2", [P, NT])
        oneh = sb("oneh", [P, NT, TOPK, E])
        chosen = sb("chosen", [P, NT, E], bf16)
        eidx = sb("eidx", [P, E])
        full = sb("full", [P, NT])
        tidx = sb("tidx", [P, NS])
        lower = sb("lower", [P, E, E])
        more = sb("more", [P, E, NT])
        ntile = sb("ntile", [P, E])
        prior = sb("prior", [P, E, E])
        first = sb("first", [P, E])
        endt = sb("endt", [P, E])
        count = sb("count", [P, E])
        grows = sb("grows", [P, E - 1])
        begin = sb("begin", [P, E])
        part = sb("part", [P, 1])
        known = sb("known", [P, NS, E - 1])
        before = sb("before", [P, NS])
        held = sb("held", [P, NS])
        due = sb("due", [P, NS])
        starts = sb("starts", [P, NS])
        gone = sb("gone", [P, NS])
        bound = sb("bound", [P, NS])
        window = sb("window", [P, NS], i32)
        owner = sb("owner", [P, RING])
        place = sb("place", [P, NT, E])
        placed = sb("placed", [P, NT, TOPK, E])
        slotf = sb("slotf", [P, NT, TOPK])
        slot = sb("slot", [P, NT, TOPK], i32)
        past = sb("past", [P, NS, E - 1])
        texf = sb("texf", [P, NS])
        tex = sb("tex", [P, NS], i32)
        wsh = sb("wsh", [P, SH, WCOLS])
        bsh = sb("bsh", [P, 2, SH])
        shg = sb("shg", [P, 2, 4 * P])
        shy = sb("shy", [P, SH, NT * P])
        base = x1_sb
        xr = sb("xr", [P, RING, ROW])
        dest = sb("dest", [P, NS], i32)
        xrT = sb("xrT", [P, 2, KD, P])
        gub = sb("gub", [P, 2, 2 * F])
        gl = sb("gl", [P, 2, F])
        yr = sb("yr", [P, 2, F])
        yrT = sb("yrT", [P, 2, P])
        rr = x_sb[:, 0:RING, :]
        res = h0

        SS, AMAX, VAR, RINV, LIM, INV, SCALE, DEQ = range(8)

        S = [ps(f"S{i}", [P, 512]) for i in range(2)]
        T = [ps(f"T{i}", [P, 512]) for i in range(2)]
        M = [ps(f"M{i}", [P, 1024]) for i in range(2)]

        def T_f(i, n):
            return T[i][:, 0:n * P].rearrange("p (k m) -> p k m", m=P)

        def group(names):
            return (sem(n) for n in names.split())

        d_idx, d_x, d_w1, d_w2, d_b, d_bx, d_wa, d_wsh, d_empty, d_brow, d_bd = group("d_idx d_x d_w1 d_w2 d_b d_bx d_wa d_wsh d_empty d_brow d_bd")
        d_cond0 = sems("d_cond0_", NT)
        d_cond1, d_scatter, d_out = group("d_cond1 d_scatter d_out")
        d_we, d_xr, d_rr = sems("d_we", E), sems("d_xr", RING), sems("d_rr", RING)
        d_pick = sems("d_pick", NT)
        p_const, p_pow, p_blk1, p_xb, p_own, p_sum, p_rq0 = group("p_const p_pow p_blk1 p_xb p_own p_sum p_rq0")
        v_own, v_empty, v_row, v_blk0, v_mean, v_h0, v_max0, v_var, v_scale = group(
            "v_own v_empty v_row v_blk0 v_mean v_h0 v_max0 v_var v_scale")
        v_turned, v_pre, v_max1, v_x1, v_chosen, v_second, v_prob, v_count, v_slot, v_window, v_tex = group(
            "v_turned v_pre v_max1 v_x1 v_chosen v_second v_prob v_count v_slot v_window v_tex")
        v_shy, v_base, v_rr, v_dest, v_gub, v_yr = group("v_shy v_base v_rr v_dest v_gub v_yr")
        v_res = sems("v_res", NT)
        a_sign, a_sq0, a_gelu, a_sq1, a_rq1, a_y, a_aff, a_shg, a_gl, a_yrT, a_xrT, a_abs, a_scaled, a_taken = group(
            "a_sign a_sq0 a_gelu a_sq1 a_rq1 a_y a_aff a_shg a_gl a_yrT a_xrT a_abs a_scaled a_taken")
        t_mean, t_c0, t_turn, t_mm1, t_mm2, t_c1, t_logit, t_rank, t_tot = group(
            "t_mean t_c0 t_turn t_mm1 t_mm2 t_c1 t_logit t_rank t_tot")
        t_sh, t_base, t_xr, t_gu, t_yr, t_dn = group("t_sh t_base t_xr t_gu t_yr t_dn")

        P_ALL = 13

        HALF = NT // 2
        LAG_UP, LAG_GELU, LAG_MAX, LAG_Q1, LAG_TURN, LAG_DOWN, LAG_C1, LAG_YT, LAG_LOGIT, LAG_RANK = 1, 2, 3, 7, 8, 9, 10, 11, 12, 13
        STEPS = NT + LAG_RANK - 1

        def second_half(i):
            return range(HALF + 2 * i, HALF + 2 * i + 2) if i < 2 else ()

        def at(i, lag):
            return i - lag if 0 <= i - lag < NT else None

        turns = {}
        for i in range(STEPS):
            for kind, lag in (("q0", 0), ("q1a", LAG_TURN), ("q1b", LAG_TURN), ("y", LAG_YT)):
                if at(i, lag) is not None:
                    turns[kind, at(i, lag)] = len(turns)
        taken = {}
        for kind, g in turns:
            by_scalar = kind == "q0"
            taken[kind, g] = (a_taken, g + 1) if by_scalar else (v_turned, 1 + sum(k != "q0" for k, _ in taken))
        taken_turn = [taken[use] for use in turns]

        block = ctx.enter_context(nc.Block())

        @block.sync
        def _(sp):
            sp.dma_start(idx_sb[:, :, :], idx.partition_broadcast(P)).then_inc(d_idx, 16)
            sp.dma_start(w1_sb, w1t.rearrange("(k p) o -> p k o", p=P)).then_inc(d_w1, 16)
            sp.wait_ge(d_cond0[HALF - 1], 16)
            sp.dma_start(w2_sb, w2t.rearrange("(k p) o -> p k o", p=P)).then_inc(d_w2, 16)
            sp.dma_start(b1_sb[:, :], b1.partition_broadcast(P)).then_inc(d_b, 16)
            sp.dma_start(wa_sb[:, :, :], wa.rearrange("(k p) e -> p k e", p=P)).then_inc(d_wa, 16)
            for e in range(SH):
                sp.dma_start(wsh[:, e, :], wshared[e]).then_inc(d_wsh, 16)
            sp.dma_start(bsh[:, :, :], bshared).then_inc(d_wsh, 16)
            sp.wait_ge(v_empty, 1)
            sp.wait_ge(t_c0, NT)
            sp.dma_start(slot_in.rearrange("(e p) d -> p e d", p=REGION)[0:P],
                         empty[:, :, :].to_broadcast([P, E, ROW])).then_inc(d_empty, 16)
            sp.wait_ge(a_sign, 2)
            sp.wait_ge(a_abs, 2)
            sp.dma_start(brow, brouted.partition_broadcast(P)).then_inc(d_brow, 16)
            for e in range(E):
                last = ((e + 1) * WCOLS - 1) // F1
                sp.wait_ge(a_rq1, min(last + 1, NT))
                if last >= NT:
                    sp.wait_ge(a_gelu, NT)
                if last >= NT + 2:
                    sp.wait_ge(t_turn, turns["q1b", NT - 1] + 1)
                sp.dma_start(wres[:, e, :], wrouted[e]).then_inc(d_we[e], 16)
            sp.dma_start(bdown_sb[:, :, :], bdown.partition_broadcast(P)).then_inc(d_bd, 16)

            def load(t, s, n, row):
                if n:
                    sp.wait_ge(t_xr, t - RING + 1)
                    sp.wait_ge(v_dest, t - RING + 1)
                sp.dma_start(xr[:, s, :], slot_in[bass.ds(row, P), :]).then_inc(d_xr[s], 16)

            sp.wait_ge(d_scatter, 16 * NT * TOPK)
            sp.wait_ge(v_window, 1)
            for t in range(NS):
                if t % 8 == 0:
                    rows = nc.values_load_multi_w_load_instructions(
                        window[0:1, t:min(t + 8, NS)], engines=[mybir.EngineType.SP], min_val=0, max_val=E * REGION - P,
                        skip_runtime_bounds_check_because="an expert has at most as many tokens as its region has slots")[1]
                load(t, t % RING, t // RING, rows[t % 8])
            for s in range(RING):
                sp.wait_ge(d_rr[s], 16 * len(range(s, NS, RING)))
            for g in range(NT):
                sp.dma_start(picked[:, g, :], token_out[g * P * TOPK:(g + 1) * P * TOPK, :].rearrange("(p k) d -> p (k d)", k=TOPK)
                             ).then_inc(d_pick[g], 16)
            for g in sorted(range(NT), key=lambda g: g + 1.5 * (g in POOL_SUMS)):
                sp.wait_ge(v_res[g], 1)
                sp.dma_start(out[g * P:(g + 1) * P, :], res[:, g, :]).then_inc(d_out, 16)
            sp.wait_ge(d_out, 16 * NT)

        @block.gpsimd
        def _(pool):
            nc.gpsimd.iota(pidx[:, :], [[0, 1]], base=0, channel_multiplier=1).then_inc(p_const, 1)
            own = 0

            def made(ins):
                nonlocal own
                own += 1
                ins.then_inc(p_own, 1)
                pool.wait_ge(p_own, own)

            made(nc.gpsimd.memset(blkmask[:, :], 1.0))
            made(nc.gpsimd.affine_select(out=blkmask[:, :], in_=blkmask[:, :], pattern=[[-C, BT]], compare_op=ALU.is_ge,
                                         fill=0.0, base=0, channel_multiplier=1))
            nc.gpsimd.affine_select(out=blkmask[:, :], in_=blkmask[:, :], pattern=[[C, BT]], compare_op=ALU.is_ge,
                                    fill=0.0, base=C - 1, channel_multiplier=-1).then_inc(p_const, 1)
            pool.wait_ge(v_row, 1)
            for g in range(NT):
                nc.gpsimd.indirect_dma_start(cond0[:, g, :], None, table0,
                                             bass.IndirectOffsetOnAxis(ap=rowidx[:, 0, g:g + 1], axis=0)).then_inc(d_cond0[g], 16)
            made(nc.gpsimd.memset(ident_f[:, :], 0.0))
            nc.gpsimd.affine_select(out=ident_f[:, :], in_=ident_f[:, :], pattern=[[-1, P]], compare_op=ALU.not_equal,
                                    fill=1.0, base=0, channel_multiplier=1).then_inc(p_const, 1)
            nc.gpsimd.memset(halfneg[:, :], -0.5).then_inc(p_const, 1)

            def inverse_root(layer, half):
                c = slice(half * HALF, (half + 1) * HALF)
                pool.wait_ge(v_var, 2 * layer + half + 1)
                nc.gpsimd.tensor_tensor(st[layer][:, RINV, c], st[layer][:, VAR, c], halfneg[:, c], ALU.pow).then_inc(p_pow, 1)

            pool.wait_ge(p_const, 4)
            inverse_root(0, 0)

            for g in range(NT):
                pool.wait_ge(v_scale, g // HALF + 1)
                if g >= 2:
                    pool.wait_ge(t_turn, turns["q0", g - 2] + 1)
                nc.gpsimd.tensor_scalar(rq0[:, g % 2, :], h0[:, g, :], st[0][:, SCALE, g:g + 1], MAGIC, ALU.mult, ALU.add).then_inc(p_rq0, 1)
                nc.gpsimd.indirect_dma_start(cond1[:, g, :], None, table1,
                                             bass.IndirectOffsetOnAxis(ap=rowidx[:, 1, g:g + 1], axis=0)).then_inc(d_cond1, 16)
                if g == HALF - 2:
                    inverse_root(0, 1)
            made(nc.gpsimd.memset(before_b[:, :], 0.0))
            nc.gpsimd.affine_select(out=before_b[:, :], in_=before_b[:, :], pattern=[[-1, P]], compare_op=ALU.is_ge,
                                    fill=1.0, base=0, channel_multiplier=1).then_inc(p_const, 1)
            made(nc.gpsimd.memset(lower[:, :, :], 0.0))
            nc.gpsimd.affine_select(out=lower[:, :, :], in_=lower[:, :, :], pattern=[[-1, E], [1, E]], compare_op=ALU.is_ge,
                                    fill=1.0, base=0, channel_multiplier=0).then_inc(p_const, 1)
            nc.gpsimd.iota(eidx[:, :], [[1, E]], base=0, channel_multiplier=0,
                           allow_small_or_imprecise_dtypes=True).then_inc(p_const, 1)
            nc.gpsimd.iota(tidx[:, :], [[1, NS]], base=0, channel_multiplier=0,
                           allow_small_or_imprecise_dtypes=True).then_inc(p_const, 1)
            nc.gpsimd.iota(full[:, :], [[P, NT]], base=0, channel_multiplier=0,
                           allow_small_or_imprecise_dtypes=True).then_inc(p_const, 1)
            nc.gpsimd.iota(y_sb[:, :, PLACE], [[TOPK * P, NT]], base=0, channel_multiplier=TOPK,
                           allow_small_or_imprecise_dtypes=True).then_inc(p_const, 1)
            nc.gpsimd.iota(spare[:, :], [[P, NS]], base=TOPK * P * NT, channel_multiplier=1,
                           allow_small_or_imprecise_dtypes=True).then_inc(p_const, 1)
            nc.gpsimd.iota(begin[:, :], [[REGION, E]], base=P, channel_multiplier=0,
                           allow_small_or_imprecise_dtypes=True).then_inc(p_const, 1)
            nc.gpsimd.iota(part[:, :], [[0, 1]], base=0, channel_multiplier=1,
                           allow_small_or_imprecise_dtypes=True).then_inc(p_const, 1)
            inverse_root(1, 0)
            pool.wait_ge(d_cond1, 16 * NT)
            for g in range(NT):
                nc.gpsimd.tensor_tensor(blk1[:, g, :].rearrange("p (q c) -> p q c", q=BT),
                                        cond1[:, g, :].unsqueeze(1).to_broadcast([P, BT, C]),
                                        blkmask[:, :].unsqueeze(2).to_broadcast([P, BT, C]), ALU.mult).then_inc(p_blk1, 1)
            pool.wait_ge(d_bx, 16)
            pool.wait_ge(d_x, 32)
            for g in range(NT):
                nc.gpsimd.tensor_tensor(base[:, g, :], x_sb[:, g, :], b2_sb[:, :], ALU.add).then_inc(p_xb, 1)
            inverse_root(1, 1)

            pool.wait_ge(d_empty, 16)
            for g in range(NT):
                if g % GROUP == 0:
                    pool.wait_ge(v_slot, g // GROUP + 1)
                    pool.wait_ge(v_second, g // GROUP + 1)
                pool.wait_ge(a_y, g + 1)
                for k in range(TOPK):
                    nc.gpsimd.indirect_dma_start(slot_in, bass.IndirectOffsetOnAxis(ap=slot[:, g, k:k + 1], axis=0),
                                                 y_sb[:, g, :], None).then_inc(d_scatter, 16)

            def send(t, s):
                pool.wait_ge(v_rr, t + 1)
                pool.wait_ge(v_dest, t + 1)
                nc.gpsimd.indirect_dma_start(token_out, bass.IndirectOffsetOnAxis(ap=dest[:, t:t + 1], axis=0),
                                             rr[:, s, :], None).then_inc(d_rr[s], 16)

            def sum_rows(g):
                made(nc.gpsimd.tensor_tensor(base[:, g, :], x1_sb[:, g, :], y_sb[:, g, 0:D], ALU.add))

            def sum_bias(g):
                nc.gpsimd.tensor_tensor(base[:, g, :], base[:, g, :], bshared_sum[:, :], ALU.add).then_inc(p_sum, 1)

            pool.wait_ge(d_bd, 16)
            made(nc.gpsimd.tensor_tensor(bshared_sum[:, :], bdown_sb[:, E, :], bdown_sb[:, E + 1, :], ALU.add))
            for t in range(NS):
                send(t, t % RING)
                if t < 2 * NT:
                    (sum_rows, sum_bias)[t % 2](t // 2)

            for n, g in enumerate(POOL_SUMS):
                pool.wait_ge(v_base, g + 1)
                pool.wait_ge(a_scaled, n + 1)
                made(nc.gpsimd.tensor_tensor(base[:, g, :], base[:, g, :], picked[:, g, 0:D], ALU.add))
                nc.gpsimd.tensor_tensor(res[:, g, :], base[:, g, :], picked[:, g, D:2 * D], ALU.add).then_inc(v_res[g], 1)

        @block.scalar
        def _(act):
            act.dma_start(x_sb[:, 0:HALF, :], x[0:HALF * P].rearrange("(g p) d -> p g d", p=P)).then_inc(d_x, 16)
            act.dma_start(x_sb[:, HALF:NT, :], x[HALF * P:].rearrange("(g p) d -> p g d", p=P)).then_inc(d_x, 16)
            act.dma_start(b2_sb[:, :], b2.partition_broadcast(P)).then_inc(d_bx, 16)
            act.wait_ge(v_empty, 2)
            act.wait_ge(d_w1, 16)
            nc.scalar.activation(w1s[:, :, :], w1_sb, ACT.Sign).then_inc(a_sign, 1)

            def abs_sum(n, w):
                nc.scalar.activation(hid[:, 2 * n:2 * n + 2, :].rearrange("p g n -> p (g n)"), w.rearrange("p k o -> p (k o)"), ACT.Abs,
                                     accum_out=wabs[:, n:n + 1]).then_inc(a_abs, 1)

            abs_sum(0, w1_sb)

            def square0(g):
                act.wait_ge(v_h0, g + 1)
                if g >= 2:
                    act.wait_ge(a_sq0, g - 1)
                nc.scalar.activation(junk0[:, g % 2, :], h0[:, g, :], ACT.Square, accum_out=st[0][:, SS, g:g + 1]).then_inc(a_sq0, 1)

            for g in range(HALF):
                square0(g)
            act.wait_ge(d_w2, 16)
            abs_sum(1, w2_sb)
            for i in range(STEPS):
                if (g := at(i, 0)) is not None:
                    u = turns["q0", g]
                    act.wait_ge(t_turn, u + 1)
                    if g >= 2:
                        act.wait_ge(t_mm1, g - 1)
                    nc.scalar.activation(qT0[:, g % 2, :, :], T_f(u % 2, KD), ACT.Copy, bias=-MAGIC).then_inc(a_taken, 1)
                for g in second_half(i):
                    square0(g)
                if (g := at(i, LAG_GELU)) is not None:
                    act.wait_ge(v_pre, g + 1)
                    nc.scalar.activation(hid[:, g, :], pre[:, g % 2, :], ACT.Gelu).then_inc(a_gelu, 1)
                    act.wait_ge(a_gelu, g + 1)
                    nc.scalar.activation(junk[:, :], hid[:, g, :], ACT.Square, accum_out=st[1][:, SS, g:g + 1]).then_inc(a_sq1, 1)
                if (g := at(i, LAG_Q1)) is not None:
                    act.wait_ge(v_scale, g // HALF + 3)
                    if g >= 2:
                        act.wait_ge(t_turn, turns["q1b", g - 2] + 1)
                    nc.scalar.activation(rq[:, g % 2, :], hid[:, g, :], ACT.Copy, bias=MAGIC,
                                         scale=st[1][:, SCALE, g:g + 1]).then_inc(a_rq1, 1)
                    if g == NT - 1:
                        nc.scalar.activation(warm[:, 0:1], ones_f[:, 0:1], ACT.Sigmoid)
                if (g := at(i, LAG_C1)) is not None:
                    act.wait_ge(t_c1, g + 1)
                    nc.scalar.activation(y_sb[:, g, 0:D], S[1][:, 0:D], ACT.Copy).then_inc(a_y, 1)
                if (g := at(i, LAG_LOGIT)) is not None and g % GROUP == GROUP - 1:
                    act.wait_ge(t_logit, g + 1)
                    nc.scalar.activation(aff[:, g - GROUP + 1:g + 1, :], M[1][:, 0:GROUP * E].rearrange("p (g e) -> p g e", e=E),
                                         ACT.Sigmoid).then_inc(a_aff, 1)
                if i == 0:
                    act.wait_ge(a_abs, 2)
                    nc.scalar.activation(w2s[:, :, :], w2_sb, ACT.Sign).then_inc(a_sign, 1)
            nc.scalar.activation(warm[:, 1:2], ones_f[:, 0:1], ACT.Gelu)
            act.wait_ge(d_wsh, 16 * (SH + 1))
            for n in range(2 * SH):
                act.wait_ge(t_sh, n + 1)
                if n >= 2:
                    act.wait_ge(v_shy, n - 1)
                nc.scalar.activation(shg[:, n % 2, :], M[n % 2][:, 0:4 * P], ACT.Gelu,
                                     bias=bsh[:, 0, n % SH:n % SH + 1]).then_inc(a_shg, 1)

            def rows_turned(t, b, first):
                act.wait_ge(t_xr, t + 1)
                if not first:
                    act.wait_ge(t_gu, t - 1)
                nc.scalar.activation(xrT[:, b, :, :], T_f(b, KD), ACT.Copy).then_inc(a_xrT, 1)

            def gate(t, b, first):
                act.wait_ge(v_gub, t + 1)
                if not first:
                    act.wait_ge(v_yr, t - 1)
                nc.scalar.activation(gl[:, b, :], gub[:, b, 0:F], ACT.Gelu).then_inc(a_gl, 1)

            def turned(t, b, first):
                act.wait_ge(t_yr, t + 1)
                if not first:
                    act.wait_ge(t_dn, t - 1)
                nc.scalar.activation(yrT[:, b, :], M[1][:, b * 512:b * 512 + P], ACT.Copy).then_inc(a_yrT, 1)

            rows_turned(0, 0, True)
            for i in range(NS + 2):
                if (t := i + 1) < NS:
                    rows_turned(t, t % 2, t < 2)
                if 0 <= (t := i - 2) < NS:
                    turned(t, t % 2, t < 2)
                if (t := i) < NS:
                    gate(t, t % 2, t < 2)

            act.wait_ge(v_prob, 1)
            for g in POOL_SUMS:
                act.wait_ge(d_pick[g], 16)
                for k in range(TOPK):
                    last = nc.scalar.activation(picked[:, g, k * D:(k + 1) * D], picked[:, g, k * D:(k + 1) * D], ACT.Copy,
                                                scale=prob[:, g, k:k + 1])
                last.then_inc(a_scaled, 1)

        @block.vector
        def _(dve):
            own = 0

            def then(ins):
                nonlocal own
                own += 1
                ins.then_inc(v_own, 1)
                dve.wait_ge(v_own, own)

            dve.wait_ge(p_const, 1)
            then(nc.vector.tensor_scalar(cidx[:, :], pidx[:, :], C - 1, None, ALU.bitwise_and))
            nc.vector.memset(empty[:, :, :], 0.0).then_inc(v_empty, 1)
            nc.vector.memset(ones_b[:, :], 1.0)
            nc.vector.memset(ones_f[:, :], 1.0).then_inc(v_empty, 1)
            dve.wait_ge(d_idx, 16)
            for b in range(BT):
                r = slice(b * C, (b + 1) * C)
                last = nc.vector.tensor_scalar(rowidx[r, :, :], idx_sb[r, :, :].rearrange("p l (g b) -> p l g b", b=BT)[:, :, :, b],
                                               float(C), cidx[r, :], ALU.mult, ALU.add)
            last.then_inc(v_row, 1)
            dve.wait_ge(p_const, 2)

            def block0(g):
                dve.wait_ge(d_cond0[g], 16)
                nc.vector.tensor_tensor(blk0[:, g, :].rearrange("p (q c) -> p q c", q=BT),
                                        cond0[:, g, 0:C].unsqueeze(1).to_broadcast([P, BT, C]),
                                        blkmask[:, :].unsqueeze(2).to_broadcast([P, BT, C]), ALU.mult).then_inc(v_blk0, 1)

            def stats0(g):
                dve.wait_ge(t_c0, g + 1)
                nc.vector.tensor_scalar(h0[:, g, :], S[g % 2][:, 0:D], cond0[:, g, C:C + 1], None, ALU.add).then_inc(v_h0, 1)
                dve.wait_ge(v_h0, g + 1)
                nc.vector.tensor_reduce(st[0][:, AMAX, g:g + 1], h0[:, g, :], AX.X, ALU.max, apply_absolute_value=True).then_inc(v_max0, 1)

            def mean(n):
                dve.wait_ge(t_mean, n + 1)
                nc.vector.tensor_scalar(wmean[:, n:n + 1], (M[0], S[1])[n][:, n:n + 1], 1.0 / (D * F1), None, ALU.mult).then_inc(v_mean, 1)
                dve.wait_ge(v_mean, n + 1)

            def variances(layer, half, width):
                c = slice(half * HALF, (half + 1) * HALF)
                s = st[layer]
                dve.wait_ge((a_sq0, a_sq1)[layer], (half + 1) * HALF)
                nc.vector.tensor_scalar(s[:, VAR, c], s[:, SS, c], 1.0 / width, EPS_RMS, ALU.mult, ALU.add).then_inc(v_var, 1)

            def scales(layer, half, width):
                c = slice(half * HALF, (half + 1) * HALF)
                s = st[layer]
                dve.wait_ge(p_pow, 2 * layer + half + 1)
                dve.wait_ge((v_max0, v_max1)[layer], (half + 1) * HALF)
                then(nc.vector.tensor_tensor(s[:, LIM, c], s[:, AMAX, c], s[:, RINV, c], ALU.mult))
                then(nc.vector.tensor_scalar(s[:, LIM, c], s[:, LIM, c], width ** -0.5, EPS_Q, ALU.mult, ALU.max))
                then(nc.vector.reciprocal(s[:, INV, c], s[:, LIM, c]))
                then(nc.vector.tensor_scalar(s[:, INV, c], s[:, INV, c], QMAX * width ** -0.5, None, ALU.mult))
                nc.vector.tensor_tensor(s[:, SCALE, c], s[:, INV, c], s[:, RINV, c], ALU.mult).then_inc(v_scale, 1)
                then(nc.vector.tensor_scalar(s[:, DEQ, c], s[:, LIM, c], wmean[:, layer:layer + 1], 1.0 / QMAX, ALU.mult, ALU.mult))

            def turned(kind, g, dst, n, rounded):
                u = turns[kind, g]
                dve.wait_ge(t_turn, u + 1)
                if rounded:
                    nc.vector.tensor_scalar(dst, T_f(u % 2, n), -MAGIC, None, ALU.add).then_inc(v_turned, 1)
                else:
                    nc.vector.tensor_copy(dst, T_f(u % 2, n)).then_inc(v_turned, 1)

            block0(0)
            block0(1)
            for g in range(HALF):
                if g + 2 < NT:
                    block0(g + 2)
                stats0(g)
            mean(0)
            variances(0, 0, D)
            scales(0, 0, D)
            for g in range(HALF + 2, NT):
                block0(g)
            def shared(n):
                dve.wait_ge(a_shg, n + 1)
                nc.vector.scalar_tensor_tensor(shy[:, n % SH, (n // SH) * 4 * P:(n // SH + 1) * 4 * P], M[n % 2][:, 4 * P:8 * P],
                                               bsh[:, 1, n % SH:n % SH + 1], shg[:, n % 2, :], ALU.add, ALU.mult).then_inc(v_shy, 1)

            def choose(q):
                c = range(q * GROUP, (q + 1) * GROUP)
                G = slice(q * GROUP, (q + 1) * GROUP)
                dve.wait_ge(a_aff, q + 1)
                for g in c:
                    last = nc.vector.max(top[:, g, :], aff[:, g, :])
                then(last)
                for g in c:
                    last = nc.vector.max_index(topi[:, g, :], top[:, g, :], aff[:, g, :])
                then(last)
                then(nc.vector.tensor_copy(topf[:, G, :], topi[:, G, 0:TOPK]))
                dve.wait_ge(p_const, P_ALL)
                then(nc.vector.tensor_tensor(oneh[:, G, :, :], topf[:, G, :].unsqueeze(3).to_broadcast([P, GROUP, TOPK, E]),
                                             eidx[:, :].unsqueeze(1).unsqueeze(1).to_broadcast([P, GROUP, TOPK, E]), ALU.is_equal))
                nc.vector.tensor_tensor(chosen[:, G, :], oneh[:, G, 0, :], oneh[:, G, 1, :], ALU.add).then_inc(v_chosen, 1)
                nc.vector.tensor_copy(y_sb[:, G, SECOND], topf[:, G, 1]).then_inc(v_second, 1)

            def slots(q):
                G = slice(q * GROUP, (q + 1) * GROUP)
                dve.wait_ge(t_rank, q + 1)
                then(nc.vector.tensor_tensor(place[:, G, :], M[1][:, 512:512 + GROUP * E].rearrange("p (g e) -> p g e", e=E),
                                             begin[:, :].unsqueeze(1).to_broadcast([P, GROUP, E]), ALU.add))
                then(nc.vector.tensor_tensor(placed[:, G, :, :], oneh[:, G, :, :],
                                             place[:, G, :].unsqueeze(2).to_broadcast([P, GROUP, TOPK, E]), ALU.mult))
                then(nc.vector.tensor_reduce(slotf[:, G, :], placed[:, G, :, :], AX.X, ALU.add))
                nc.vector.tensor_copy(slot[:, G, :], slotf[:, G, :]).then_inc(v_slot, 1)

            dve.wait_ge(d_b, 16)
            for i in range(STEPS):
                for g in second_half(i):
                    stats0(g)
                if i == 1:
                    variances(0, 1, D)
                if (g := at(i, LAG_MAX)) is not None:
                    dve.wait_ge(a_gelu, g + 1)
                    nc.vector.tensor_reduce(st[1][:, AMAX, g:g + 1], hid[:, g, :], AX.X, ALU.max, apply_absolute_value=True).then_inc(v_max1, 1)
                    if g == HALF - 1:
                        mean(1)
                    if g % HALF == HALF - 1:
                        variances(1, g // HALF, F1)
                if (g := at(i, LAG_TURN)) is not None:
                    if g >= 2:
                        dve.wait_ge(t_mm2, g - 1)
                    turned("q1a", g, qT1[:, g % 2, 0:4, :], 4, True)
                    turned("q1b", g, qT1[:, g % 2, 4:8, :], 4, True)
                if (g := at(i, LAG_UP)) is not None:
                    dve.wait_ge(t_mm1, g + 1)
                    if g >= 2:
                        dve.wait_ge(a_gelu, g - 1)
                    nc.vector.scalar_tensor_tensor(pre[:, g % 2, :], M[g % 2][:, :], st[0][:, DEQ, g:g + 1], b1_sb[:, :],
                                                   ALU.mult, ALU.add).then_inc(v_pre, 1)
                if i == 2:
                    scales(0, 1, D)
                if (g := at(i, LAG_MAX)) is not None and g % HALF == HALF - 1:
                    scales(1, g // HALF, F1)
                if (g := at(i, LAG_DOWN)) is not None:
                    dve.wait_ge(t_mm2, g + 1)
                    dve.wait_ge(p_xb, g + 1)
                    nc.vector.scalar_tensor_tensor(x1_sb[:, g, :], S[0][:, 0:D], st[1][:, DEQ, g:g + 1], base[:, g, :],
                                                   ALU.mult, ALU.add).then_inc(v_x1, 1)
                if (g := at(i, LAG_YT)) is not None:
                    turned("y", g, yT_sb[:, :, g, :], KD, False)
                if (g := at(i, LAG_LOGIT)) is not None and g % GROUP == GROUP - 1:
                    choose(g // GROUP)
                if (g := at(i, LAG_RANK)) is not None and g % GROUP == GROUP - 1:
                    slots(g // GROUP)

            then(nc.vector.tensor_tensor(psum2[:, :], top[:, :, 0], top[:, :, 1], ALU.add))
            then(nc.vector.reciprocal(psum2[:, :], psum2[:, :]))
            nc.vector.tensor_tensor(prob[:, :, :], top[:, :, 0:TOPK], psum2[:, :].unsqueeze(2).to_broadcast([P, NT, TOPK]), ALU.mult).then_inc(v_prob, 1)
            slots(NT // GROUP - 1)
            dve.wait_ge(t_tot, 1)
            nc.vector.tensor_copy(count[:, :], S[1][:, 0:E]).then_inc(v_count, 1)
            dve.wait_ge(v_count, 1)
            nc.vector.tensor_tensor(grows[:, :], count[:, 1:E], count[:, 0:E - 1], ALU.subtract)
            then(nc.vector.tensor_tensor(more[:, :, :], count[:, :].unsqueeze(2).to_broadcast([P, E, NT]),
                                         full[:, :].unsqueeze(1).to_broadcast([P, E, NT]), ALU.is_gt))
            then(nc.vector.tensor_reduce(ntile[:, :], more[:, :, :], AX.X, ALU.add))
            then(nc.vector.tensor_tensor(prior[:, :, :], ntile[:, :].unsqueeze(1).to_broadcast([P, E, E]), lower[:, :, :], ALU.mult))
            then(nc.vector.tensor_reduce(first[:, :], prior[:, :, :], AX.X, ALU.add))
            then(nc.vector.tensor_tensor(endt[:, :], first[:, :], ntile[:, :], ALU.add))
            then(nc.vector.tensor_tensor(past[:, :, :], endt[:, 0:E - 1].unsqueeze(1).to_broadcast([P, NS, E - 1]),
                                         tidx[:, :].unsqueeze(2).to_broadcast([P, NS, E - 1]), ALU.is_le))
            nc.vector.tensor_reduce(texf[:, :], past[:, :, :], AX.X, ALU.add)
            shared(0)
            then(nc.vector.tensor_tensor(known[:, :, :], past[:, :, :], ntile[:, 0:E - 1].unsqueeze(1).to_broadcast([P, NS, E - 1]), ALU.mult))
            then(nc.vector.tensor_reduce(before[:, :], known[:, :, :], AX.X, ALU.add))
            shared(1)
            then(nc.vector.tensor_tensor(due[:, :], tidx[:, :], before[:, :], ALU.subtract))
            nc.vector.tensor_scalar(due[:, :], due[:, :], float(P), None, ALU.mult)
            then(nc.vector.tensor_tensor(known[:, :, :], past[:, :, :], grows[:, :].unsqueeze(1).to_broadcast([P, NS, E - 1]), ALU.mult))
            then(nc.vector.tensor_reduce(held[:, :], known[:, :, :], AX.X, ALU.add))
            then(nc.vector.tensor_scalar(held[:, :], held[:, :], count[:, 0:1], -float(P), ALU.add, ALU.add))
            then(nc.vector.tensor_tensor(starts[:, :], due[:, :], held[:, :], ALU.min))
            nc.vector.tensor_tensor(gone[:, :], due[:, :], starts[:, :], ALU.subtract)
            then(nc.vector.tensor_scalar(starts[:, :], starts[:, :], float(P), None, ALU.add))
            nc.vector.scalar_tensor_tensor(window[:, :], texf[:, :], float(REGION), starts[:, :], ALU.mult, ALU.add).then_inc(v_window, 1)
            then(nc.vector.scalar_tensor_tensor(bound[:, :], gone[:, :], part[:, :], spare[:, :], ALU.is_gt, ALU.mult))
            nc.vector.tensor_copy(tex[:, :], texf[:, :]).then_inc(v_tex, 1)
            shared(2)
            shared(3)


            def rest(g):
                dve.wait_ge(t_base, g + 1)
                dve.wait_ge(p_sum, g + 1)
                nc.vector.tensor_tensor(base[:, g, :], base[:, g, :], T[g % 2][:, 0:D], ALU.add).then_inc(v_base, 1)

            def experts(t, n):
                return nc.values_load_multi_w_load_instructions(
                    tex[0:1, t:t + n], engines=[mybir.EngineType.DVE], min_val=0, max_val=E - 1,
                    skip_runtime_bounds_check_because="the routing keeps it below the number of experts")[1]

            def places(t, s):
                dve.wait_ge(d_xr[s], 16 * (t // RING + 1))
                then(nc.vector.scalar_tensor_tensor(owner[:, s:s + 1], xr[:, s, SECOND:PLACE], texf[:, t:t + 1],
                                                    xr[:, s, PLACE:ROW], ALU.is_equal, ALU.add))
                nc.vector.tensor_tensor(dest[:, t:t + 1], owner[:, s:s + 1], bound[:, t:t + 1], ALU.max).then_inc(v_dest, 1)

            def biased(t, b, e, first):
                dve.wait_ge(t_gu, t + 1)
                if not first:
                    dve.wait_ge(a_gl, t - 1)
                nc.vector.tensor_tensor(gub[:, b, :], M[0][:, b * 512:b * 512 + 2 * F],
                                        brow[:, bass.ds(e, 1), :].rearrange("p a n -> p (a n)"), ALU.add).then_inc(v_gub, 1)

            def gated(t, b, first):
                dve.wait_ge(a_gl, t + 1)
                if not first:
                    dve.wait_ge(t_yr, t - 1)
                nc.vector.tensor_tensor(yr[:, b, :], gub[:, b, F:2 * F], gl[:, b, :], ALU.mult).then_inc(v_yr, 1)

            def rows(t, b, s, n, e):
                dve.wait_ge(t_dn, t + 1)
                if n:
                    dve.wait_ge(d_rr[s], 16 * n)
                nc.vector.tensor_tensor(rr[:, s, :], S[b][:, 0:D], bdown_sb[:, bass.ds(e, 1), :].rearrange("p a n -> p (a n)"),
                                        ALU.add).then_inc(v_rr, 1)

            dve.wait_ge(d_brow, 16)
            dve.wait_ge(d_bd, 16)
            ex = {}
            dve.wait_ge(v_tex, 1)
            for i in range(-1, NS + 3):
                if 0 <= i < NS and i % 8 == 0:
                    n = min(8, NS - i)
                    ex.update(zip(range(i, i + n), experts(i, n)))
                if 0 <= (t := i + 1) < NS:
                    places(t, t % RING)
                if 0 <= (t := i - 1) < NS:
                    gated(t, t % 2, t < 2)
                if 0 <= (t := i) < NS:
                    biased(t, t % 2, ex[t], t < 2)
                if 0 <= (t := i - 3) < NS:
                    rows(t, t % 2, t % RING, t // RING, ex.pop(t))

            def combine(g):
                dve.wait_ge(v_base, g + 1)
                dve.wait_ge(d_pick[g], 16)
                then(nc.vector.scalar_tensor_tensor(base[:, g, :], picked[:, g, 0:D], prob[:, g, 0:1], base[:, g, :], ALU.mult, ALU.add))
                nc.vector.scalar_tensor_tensor(res[:, g, :], picked[:, g, D:2 * D], prob[:, g, 1:2], base[:, g, :],
                                               ALU.mult, ALU.add).then_inc(v_res[g], 1)

            for g in range(NT):
                rest(g)
                if g >= LAG_SUM and g - LAG_SUM not in POOL_SUMS:
                    combine(g - LAG_SUM)
            for g in range(NT - LAG_SUM, NT):
                if g not in POOL_SUMS:
                    combine(g)

        @block.tensor
        def _(pe):
            def mm(o, l, r, start=True, stop=True):
                return nc.tensor.matmul(o, l, r, start=start, stop=stop)

            def turn(kind, g, blocks, rows=P):
                u = turns[kind, g]
                if u >= 2:
                    pe.wait_ge(*taken_turn[u - 2])
                for k, b in enumerate(blocks):
                    last = nc.tensor.transpose(T_f(u % 2, len(blocks))[0:rows, k, :], b, ident_f[:, :])
                last.then_inc(t_turn, 1)

            def mean(n):
                pe.wait_ge(a_abs, n + 1)
                mm((M[0], S[1])[n][:, n:n + 1], ones_f[:, :], wabs[:, n:n + 1]).then_inc(t_mean, 1)

            def condition0(g):
                pe.wait_ge(v_blk0, g + 1)
                if g >= 2:
                    pe.wait_ge(v_h0, g - 1)
                mm(S[g % 2][:, 0:D], blk0[:, g, :], x_sb[:, g, :]).then_inc(t_c0, 1)

            def rank(q):
                pe.wait_ge(v_chosen, q + 1)
                pe.wait_ge(p_const, P_ALL)
                if q:
                    pe.wait_ge(v_slot, q)
                R = M[1][:, 512:512 + GROUP * E].rearrange("p (g e) -> p g e", e=E)
                c = q * GROUP
                mm(R, before_b[:, :], chosen[:, c:c + GROUP, :], True, False)
                for g in range(c):
                    mm(R, ones_b[:, :], chosen[:, g, :].unsqueeze(1).to_broadcast([P, GROUP, E]), False, False)
                for s in range(1, GROUP):
                    last = mm(R[:, s:, :], ones_b[:, :], chosen[:, c:c + GROUP - s, :], False, s == GROUP - 1)
                last.then_inc(t_rank, 1)

            pe.wait_ge(v_empty, 2)
            pe.wait_ge(d_x, 32)
            for g in range(HALF):
                condition0(g)
            mean(0)
            pe.wait_ge(p_const, 3)
            pe.wait_ge(a_sign, 1)
            for i in range(STEPS):
                if (g := at(i, 0)) is not None:
                    pe.wait_ge(p_rq0, g + 1)
                    turn("q0", g, [rq0[:, g % 2, k * P:(k + 1) * P] for k in range(KD)])
                for g in second_half(i):
                    condition0(g)
                if i == HALF:
                    pe.wait_ge(v_h0, NT)
                    mean(1)
                if (g := at(i, LAG_UP)) is not None:
                    pe.wait_ge(*taken["q0", g])
                    if g >= 2:
                        pe.wait_ge(v_pre, g - 1)
                    if g == 0:
                        pe.wait_ge(v_mean, 1)
                    for n in range(2):
                        for k in range(KD):
                            last = mm(M[g % 2][:, n * 512:(n + 1) * 512], qT0[:, g % 2, k, :], w1s[:, k, n * 512:(n + 1) * 512],
                                      k == 0, k == KD - 1)
                    last.then_inc(t_mm1, 1)
                if (g := at(i, LAG_TURN)) is not None:
                    pe.wait_ge(a_rq1, g + 1)
                    for n, kind in enumerate(("q1a", "q1b")):
                        turn(kind, g, [rq[:, g % 2, k * P:(k + 1) * P] for k in range(4 * n, 4 * n + 4)])
                if (g := at(i, LAG_DOWN)) is not None:
                    pe.wait_ge(*taken["q1b", g])
                    pe.wait_ge(a_sign, 2)
                    if g:
                        pe.wait_ge(v_x1, g)
                    for k in range(KF):
                        last = mm(S[0][:, 0:D], qT1[:, g % 2, k, :], w2s[:, k, :], k == 0, k == KF - 1)
                    last.then_inc(t_mm2, 1)
                if (g := at(i, LAG_C1)) is not None:
                    pe.wait_ge(v_x1, g + 1)
                    pe.wait_ge(p_blk1, g + 1)
                    if g:
                        pe.wait_ge(a_y, g)
                    else:
                        pe.wait_ge(v_mean, 2)
                    mm(S[1][:, 0:D], blk1[:, g, :], x1_sb[:, g, :]).then_inc(t_c1, 1)
                if (g := at(i, LAG_YT)) is not None:
                    pe.wait_ge(a_y, g + 1)
                    turn("y", g, [y_sb[:, g, k * P:(k + 1) * P] for k in range(KD)])
                if (g := at(i, LAG_LOGIT)) is not None:
                    pe.wait_ge(*taken["y", g])
                    pe.wait_ge(v_pre, NT)
                    pe.wait_ge(d_wa, 16)
                    if g >= GROUP:
                        pe.wait_ge(a_aff, g // GROUP)
                    for k in range(KD):
                        last = mm(M[1][:, g % GROUP * E:(g % GROUP + 1) * E], yT_sb[:, k, g, :], wa_sb[:, k, :], k == 0, k == KD - 1)
                    last.then_inc(t_logit, 1)
                if (g := at(i, LAG_RANK)) is not None and g % GROUP == GROUP - 1:
                    rank(g // GROUP)

            pe.wait_ge(d_wsh, 16 * (SH + 1))

            def shared(n, gate):
                e, h = n % SH, n // SH
                if gate and n >= 2:
                    pe.wait_ge(v_shy, n - 1)
                elif gate and n == 1:
                    pe.wait_ge(v_slot, NT // GROUP)
                at_ = gate_at if gate else up_at
                for k in range(KD):
                    last = mm(M[n % 2][:, 0:4 * P] if gate else M[n % 2][:, 4 * P:8 * P], wsh[:, e, at_(k):at_(k) + F],
                              yT_sb[:, k, 4 * h:4 * h + 4, :], k == 0, k == KD - 1)
                if not gate:
                    last.then_inc(t_sh, 1)

            shared(0, True)
            rank(NT // GROUP - 1)
            pe.wait_ge(a_y, NT)
            for g in range(NT):
                last = mm(S[1][:, 0:E], ones_b[:, :], chosen[:, g, :], g == 0, g == NT - 1)
            last.then_inc(t_tot, 1)
            shared(0, False)
            shared(1, True)
            shared(1, False)
            for n in range(2, 2 * SH):
                shared(n, True)
                shared(n, False)

            def rest(g):
                pe.wait_ge(v_shy, SH * (g // HALF + 1))
                if g >= 2:
                    pe.wait_ge(v_base, g - 1)
                for e in range(SH):
                    last = mm(T[g % 2][:, 0:D], shy[:, e, g * P:(g + 1) * P], wsh[:, e, DO:DO + D], e == 0, e == SH - 1)
                last.then_inc(t_base, 1)

            def turn_rows(t, b, s, n, first):
                pe.wait_ge(d_xr[s], 16 * (n + 1))
                if not first:
                    pe.wait_ge(a_xrT, t - 1)
                for k in range(KD):
                    last = nc.tensor.transpose(T_f(b, KD)[:, k, :], xr[:, s, k * P:(k + 1) * P], ident_f[:, :])
                last.then_inc(t_xr, 1)

            def experts(t, n):
                return nc.values_load_multi_w_load_instructions(
                    tex[0:1, t:t + n], engines=[mybir.EngineType.PE], min_val=0, max_val=E - 1,
                    skip_runtime_bounds_check_because="the routing keeps it below the number of experts")[1]

            def up(t, b, e, first):
                pe.wait_ge(a_xrT, t + 1)
                if not first:
                    pe.wait_ge(v_gub, t - 1)
                for k in range(KD):
                    last = mm(M[0][:, b * 512:b * 512 + 2 * F], xrT[:, b, k, :],
                              wres[:, bass.ds(e, 1), gate_at(k):gate_at(k) + 2 * F].rearrange("p a n -> p (a n)"), k == 0, k == KD - 1)
                last.then_inc(t_gu, 1)

            def turn_gated(t, b, first):
                pe.wait_ge(v_yr, t + 1)
                if not first:
                    pe.wait_ge(a_yrT, t - 1)
                nc.tensor.transpose(M[1][:, b * 512:b * 512 + P], yr[:, b, :], ident_f[:, :]).then_inc(t_yr, 1)

            def down(t, b, e, first):
                pe.wait_ge(a_yrT, t + 1)
                if not first:
                    pe.wait_ge(v_rr, t - 1)
                mm(S[b][:, 0:D], yrT[:, b, :], wres[:, bass.ds(e, 1), DO:DO + D].rearrange("p a n -> p (a n)")).then_inc(t_dn, 1)

            ex = {}
            pe.wait_ge(v_tex, 1)
            for e in range(E):
                pe.wait_ge(d_we[e], 16)
            turn_rows(0, 0, 0, 0, True)
            for i in range(NS + 3):
                if i < NS and i % 8 == 0:
                    n = min(8, NS - i)
                    ex.update(zip(range(i, i + n), experts(i, n)))
                if (t := i + 1) < NS:
                    turn_rows(t, t % 2, t % RING, t // RING, t < 2)
                if i == 0:
                    pe.wait_ge(v_shy, 2 * SH)
                if (t := i) < NS:
                    up(t, t % 2, ex[t], t < 2)
                if 0 <= (t := i - 2) < NS:
                    turn_gated(t, t % 2, t < 2)
                if 0 <= (t := i - 3) < NS:
                    down(t, t % 2, ex.pop(t), t < 2)
                if i == NS - 1:
                    pe.wait_ge(a_xrT, NS)
                if i >= REST_FROM:
                    rest(i - REST_FROM)
            for g in range(NS + 3 - REST_FROM, NT):
                rest(g)


def pack_experts(g, u, d):
    n = g.shape[0]
    gu = np.stack([w.reshape(n, KD, P, F) for w in (g, u)], axis=3)
    return np.concatenate([gu.transpose(0, 2, 1, 3, 4).reshape(n, P, 2 * KD * F), d], axis=2)


def kernel(**inputs):
    import concourse.bacc as bacc
    from concourse.bass_utils import run_bass_kernel_spmd

    v = {k: np.asarray(a) for k, a in inputs.items()}
    arrays = {
        "x": v["x"].reshape(B * C, D),
        "idx": np.stack([v["itok_B_0_7"], v["itok_B_1_198"]]),
        "table0": np.concatenate([v["L0_cond_weights"].reshape(N0 * C, C), v["fside_8xS_0"].reshape(N0 * C, 1)], axis=1),
        "table1": v["L1_cond_weights"].reshape(N1 * C, C),
        "w1t": v["L0_ffn_w1"].T,
        "b1": v["L0_ffn_b1"],
        "w2t": v["L0_ffn_w2"].T,
        "b2": v["L0_ffn_b2"],
        "wa": v["L1_ffn_wa"],
        "wshared": pack_experts(*(v["L1_ffn_" + n] for n in ("sg", "sw1", "sw2"))),
        "bshared": np.stack([v["L1_ffn_sgb"].T, v["L1_ffn_sb1"].T], axis=1),
        "wrouted": pack_experts(*(v["L1_ffn_" + n] for n in ("rg", "rw1", "rw2"))),
        "brouted": np.stack([v["L1_ffn_rgb"], v["L1_ffn_rb1"]], axis=1).reshape(E, 2 * F),
        "bdown": np.concatenate([v["L1_ffn_rb2"], v["L1_ffn_sb2"]], axis=0),
    }
    arrays = {k: np.ascontiguousarray(a) for k, a in arrays.items()}
    nc = bacc.Bacc("TRN2", target_bir_lowering=False, num_devices=1)
    args = [nc.dram_tensor(k, a.shape, mybir.dt.from_np(a.dtype), kind="ExternalInput").ap() for k, a in arrays.items()]
    out = nc.dram_tensor("out", [B * C, D], mybir.dt.float32, kind="ExternalOutput").ap()
    adaln_moe(nc, *args, out)
    r = run_bass_kernel_spmd(nc, [arrays], core_ids=[0])
    return r.results[0]["out"].reshape(B, C, D)
```
